# Optimizing a Trainium2 kernel written in Bass

```python
import numpy as np
import jax
import jax.numpy as jnp

def _softmax(x, axis=-1):
    return jax.nn.softmax(x, axis=axis)

def _gelu(x):
    return jax.nn.gelu(x, approximate=True)

def _silu(x):
    return jax.nn.silu(x)

def _sigmoid(x):
    return jax.nn.sigmoid(x)

def _layernorm(x, axis=-1, eps=1e-05):
    m = jnp.mean(x, axis=axis, keepdims=True)
    v = jnp.var(x, axis=axis, keepdims=True)
    return (x - m) / jnp.sqrt(v + eps)

def _scatter_add(tgt, idx, src, axis=0):
    return tgt.at[idx].add(src)

def _segment_sum(src, seg, n):
    return jax.ops.segment_sum(src, seg, n)
kernel_name = 'mk_dlrm_tower_d1_rec_r8_0567cd'

def setup_inputs(seed: int=0):
    np.random.seed(seed)
    _w = jnp.asarray

    def _rec_inputs():
        import jax
        import jax.numpy as jnp
        _tk = jax.random.key(seed)
        dense_ctx = jax.random.normal(jax.random.fold_in(_tk, 190), (2048, 16), jnp.float32)
        ids = jnp.stack([jax.random.randint(jax.random.fold_in(_tk, 200 + f), (2048,), 0, v, jnp.int32) for f, v in enumerate([125000, 1000, 1000, 12500, 1000, 1000, 1250, 1250, 1250, 125000, 12500, 125000, 12500, 12500, 1250, 1250, 1000, 125000, 125000, 12500, 1250, 1250, 1000, 1250, 125000, 125000, 12500, 1250, 1000, 1250, 1000, 1000])], axis=1)
        tbl_0 = 0.05 * jax.random.normal(jax.random.fold_in(_tk, 500 + 0), (125000, 32), jnp.float32)
        tbl_1 = 0.05 * jax.random.normal(jax.random.fold_in(_tk, 500 + 1), (1000, 32), jnp.float32)
        tbl_2 = 0.05 * jax.random.normal(jax.random.fold_in(_tk, 500 + 2), (1000, 32), jnp.float32)
        tbl_3 = 0.05 * jax.random.normal(jax.random.fold_in(_tk, 500 + 3), (12500, 32), jnp.float32)
        tbl_4 = 0.05 * jax.random.normal(jax.random.fold_in(_tk, 500 + 4), (1000, 32), jnp.float32)
        tbl_5 = 0.05 * jax.random.normal(jax.random.fold_in(_tk, 500 + 5), (1000, 32), jnp.float32)
        tbl_6 = 0.05 * jax.random.normal(jax.random.fold_in(_tk, 500 + 6), (1250, 32), jnp.float32)
        tbl_7 = 0.05 * jax.random.normal(jax.random.fold_in(_tk, 500 + 7), (1250, 32), jnp.float32)
        tbl_8 = 0.05 * jax.random.normal(jax.random.fold_in(_tk, 500 + 8), (1250, 32), jnp.float32)
        tbl_9 = 0.05 * jax.random.normal(jax.random.fold_in(_tk, 500 + 9), (125000, 32), jnp.float32)
        tbl_10 = 0.05 * jax.random.normal(jax.random.fold_in(_tk, 500 + 10), (12500, 32), jnp.float32)
        tbl_11 = 0.05 * jax.random.normal(jax.random.fold_in(_tk, 500 + 11), (125000, 32), jnp.float32)
        tbl_12 = 0.05 * jax.random.normal(jax.random.fold_in(_tk, 500 + 12), (12500, 32), jnp.float32)
        tbl_13 = 0.05 * jax.random.normal(jax.random.fold_in(_tk, 500 + 13), (12500, 32), jnp.float32)
        tbl_14 = 0.05 * jax.random.normal(jax.random.fold_in(_tk, 500 + 14), (1250, 32), jnp.float32)
        tbl_15 = 0.05 * jax.random.normal(jax.random.fold_in(_tk, 500 + 15), (1250, 32), jnp.float32)
        tbl_16 = 0.05 * jax.random.normal(jax.random.fold_in(_tk, 500 + 16), (1000, 32), jnp.float32)
        tbl_17 = 0.05 * jax.random.normal(jax.random.fold_in(_tk, 500 + 17), (125000, 32), jnp.float32)
        tbl_18 = 0.05 * jax.random.normal(jax.random.fold_in(_tk, 500 + 18), (125000, 32), jnp.float32)
        tbl_19 = 0.05 * jax.random.normal(jax.random.fold_in(_tk, 500 + 19), (12500, 32), jnp.float32)
        tbl_20 = 0.05 * jax.random.normal(jax.random.fold_in(_tk, 500 + 20), (1250, 32), jnp.float32)
        tbl_21 = 0.05 * jax.random.normal(jax.random.fold_in(_tk, 500 + 21), (1250, 32), jnp.float32)
        tbl_22 = 0.05 * jax.random.normal(jax.random.fold_in(_tk, 500 + 22), (1000, 32), jnp.float32)
        tbl_23 = 0.05 * jax.random.normal(jax.random.fold_in(_tk, 500 + 23), (1250, 32), jnp.float32)
        tbl_24 = 0.05 * jax.random.normal(jax.random.fold_in(_tk, 500 + 24), (125000, 32), jnp.float32)
        tbl_25 = 0.05 * jax.random.normal(jax.random.fold_in(_tk, 500 + 25), (125000, 32), jnp.float32)
        tbl_26 = 0.05 * jax.random.normal(jax.random.fold_in(_tk, 500 + 26), (12500, 32), jnp.float32)
        tbl_27 = 0.05 * jax.random.normal(jax.random.fold_in(_tk, 500 + 27), (1250, 32), jnp.float32)
        tbl_28 = 0.05 * jax.random.normal(jax.random.fold_in(_tk, 500 + 28), (1000, 32), jnp.float32)
        tbl_29 = 0.05 * jax.random.normal(jax.random.fold_in(_tk, 500 + 29), (1250, 32), jnp.float32)
        tbl_30 = 0.05 * jax.random.normal(jax.random.fold_in(_tk, 500 + 30), (1000, 32), jnp.float32)
        tbl_31 = 0.05 * jax.random.normal(jax.random.fold_in(_tk, 500 + 31), (1000, 32), jnp.float32)
        _rk = jax.random.fold_in(_tk, 7)
        W_top1 = 0.0830455 * jax.random.normal(jax.random.fold_in(_tk, 801), (145, 512), jnp.float32)
        W_top2 = 0.0441942 * jax.random.normal(jax.random.fold_in(_tk, 802), (512, 256), jnp.float32)
        W_top3 = 0.0625 * jax.random.normal(jax.random.fold_in(_tk, 803), (256, 1), jnp.float32)
        b_top1 = jnp.zeros((512,), jnp.float32)
        b_top2 = jnp.zeros((256,), jnp.float32)
        return (dense_ctx, ids, tbl_0, tbl_1, tbl_2, tbl_3, tbl_4, tbl_5, tbl_6, tbl_7, tbl_8, tbl_9, tbl_10, tbl_11, tbl_12, tbl_13, tbl_14, tbl_15, tbl_16, tbl_17, tbl_18, tbl_19, tbl_20, tbl_21, tbl_22, tbl_23, tbl_24, tbl_25, tbl_26, tbl_27, tbl_28, tbl_29, tbl_30, tbl_31, W_top1, b_top1, W_top2, b_top2, W_top3)
    dense_ctx, ids, tbl_0, tbl_1, tbl_2, tbl_3, tbl_4, tbl_5, tbl_6, tbl_7, tbl_8, tbl_9, tbl_10, tbl_11, tbl_12, tbl_13, tbl_14, tbl_15, tbl_16, tbl_17, tbl_18, tbl_19, tbl_20, tbl_21, tbl_22, tbl_23, tbl_24, tbl_25, tbl_26, tbl_27, tbl_28, tbl_29, tbl_30, tbl_31, W_top1, b_top1, W_top2, b_top2, W_top3 = _rec_inputs()

    def _L0_rec_setup():
        import jax, jax.numpy as jnp
        import numpy as np

        def _cin(x, Ws, bs):
            B, F, D = x.shape
            h = x
            directs = []
            n_layers = len(Ws)
            for i, (W, b) in enumerate(zip(Ws, bs)):
                O = W.shape[0]
                H = h.shape[1]
                z = jnp.einsum('bhd,bmd,ohm->bod', h, x, W.reshape(O, H, F))
                z = jax.nn.relu(z + b[None, :, None])
                if i < n_layers - 1:
                    half = O // 2
                    h, direct = (z[:, :half, :], z[:, half:, :])
                else:
                    direct = z
                directs.append(direct)
            out = jnp.concatenate(directs, axis=1)
            return jnp.sum(out, axis=-1)
        key = jax.random.key(seed)
        ks = jax.random.split(key, 4)
        B, F, D = (256, 32, 32)
        x = jax.random.normal(ks[0], (B, F, D), dtype=jnp.float32)
        W0 = jax.random.normal(ks[1], (128, 32 * F), dtype=jnp.float32) * 0.05
        W1 = jax.random.normal(ks[2], (128, 64 * F), dtype=jnp.float32) * 0.05
        W2 = jax.random.normal(ks[3], (1, 64 * F), dtype=jnp.float32) * 0.05
        return {'x': x, 'W0': W0, 'b0': jnp.zeros((128,), jnp.float32), 'W1': W1, 'b1': jnp.zeros((128,), jnp.float32), 'W2': W2, 'b2': jnp.zeros((1,), jnp.float32)}
    _L0_rec_all = _L0_rec_setup()
    _L0_rec_in = {k: v for k, v in _L0_rec_all.items() if k in ('W0', 'b0', 'W1', 'b1', 'W2', 'b2')}
    del _L0_rec_all
    return {'dense_ctx': dense_ctx, 'ids': ids, 'tbl_0': tbl_0, 'tbl_1': tbl_1, 'tbl_2': tbl_2, 'tbl_3': tbl_3, 'tbl_4': tbl_4, 'tbl_5': tbl_5, 'tbl_6': tbl_6, 'tbl_7': tbl_7, 'tbl_8': tbl_8, 'tbl_9': tbl_9, 'tbl_10': tbl_10, 'tbl_11': tbl_11, 'tbl_12': tbl_12, 'tbl_13': tbl_13, 'tbl_14': tbl_14, 'tbl_15': tbl_15, 'tbl_16': tbl_16, 'tbl_17': tbl_17, 'tbl_18': tbl_18, 'tbl_19': tbl_19, 'tbl_20': tbl_20, 'tbl_21': tbl_21, 'tbl_22': tbl_22, 'tbl_23': tbl_23, 'tbl_24': tbl_24, 'tbl_25': tbl_25, 'tbl_26': tbl_26, 'tbl_27': tbl_27, 'tbl_28': tbl_28, 'tbl_29': tbl_29, 'tbl_30': tbl_30, 'tbl_31': tbl_31, 'W_top1': W_top1, 'b_top1': b_top1, 'W_top2': W_top2, 'b_top2': b_top2, 'W_top3': W_top3, 'L0_rec_W0': _L0_rec_in['W0'], 'L0_rec_b0': _L0_rec_in['b0'], 'L0_rec_W1': _L0_rec_in['W1'], 'L0_rec_b1': _L0_rec_in['b1'], 'L0_rec_W2': _L0_rec_in['W2'], 'L0_rec_b2': _L0_rec_in['b2']}

def reference(dense_ctx, ids, tbl_0, tbl_1, tbl_2, tbl_3, tbl_4, tbl_5, tbl_6, tbl_7, tbl_8, tbl_9, tbl_10, tbl_11, tbl_12, tbl_13, tbl_14, tbl_15, tbl_16, tbl_17, tbl_18, tbl_19, tbl_20, tbl_21, tbl_22, tbl_23, tbl_24, tbl_25, tbl_26, tbl_27, tbl_28, tbl_29, tbl_30, tbl_31, W_top1, b_top1, W_top2, b_top2, W_top3, L0_rec_W0, L0_rec_b0, L0_rec_W1, L0_rec_b1, L0_rec_W2, L0_rec_b2):
    import jax
    import jax.numpy as jnp

    def _L0_rec_ref(x, W0, b0, W1, b1, W2, b2):
        import jax, jax.numpy as jnp
        import numpy as np

        def _cin(x, Ws, bs):
            B, F, D = x.shape
            h = x
            directs = []
            n_layers = len(Ws)
            for i, (W, b) in enumerate(zip(Ws, bs)):
                O = W.shape[0]
                H = h.shape[1]
                z = jnp.einsum('bhd,bmd,ohm->bod', h, x, W.reshape(O, H, F))
                z = jax.nn.relu(z + b[None, :, None])
                if i < n_layers - 1:
                    half = O // 2
                    h, direct = (z[:, :half, :], z[:, half:, :])
                else:
                    direct = z
                directs.append(direct)
            out = jnp.concatenate(directs, axis=1)
            return jnp.sum(out, axis=-1)
        return _cin(x, (W0, W1, W2), (b0, b1, b2))
    e = jnp.stack([tbl_0[ids[:, 0]], tbl_1[ids[:, 1]], tbl_2[ids[:, 2]], tbl_3[ids[:, 3]], tbl_4[ids[:, 4]], tbl_5[ids[:, 5]], tbl_6[ids[:, 6]], tbl_7[ids[:, 7]], tbl_8[ids[:, 8]], tbl_9[ids[:, 9]], tbl_10[ids[:, 10]], tbl_11[ids[:, 11]], tbl_12[ids[:, 12]], tbl_13[ids[:, 13]], tbl_14[ids[:, 14]], tbl_15[ids[:, 15]], tbl_16[ids[:, 16]], tbl_17[ids[:, 17]], tbl_18[ids[:, 18]], tbl_19[ids[:, 19]], tbl_20[ids[:, 20]], tbl_21[ids[:, 21]], tbl_22[ids[:, 22]], tbl_23[ids[:, 23]], tbl_24[ids[:, 24]], tbl_25[ids[:, 25]], tbl_26[ids[:, 26]], tbl_27[ids[:, 27]], tbl_28[ids[:, 28]], tbl_29[ids[:, 29]], tbl_30[ids[:, 30]], tbl_31[ids[:, 31]]], axis=1)
    z = _L0_rec_ref(e, L0_rec_W0, L0_rec_b0, L0_rec_W1, L0_rec_b1, L0_rec_W2, L0_rec_b2)
    z = z.reshape(z.shape[0], -1)
    h = jnp.concatenate([z, dense_ctx], axis=1)
    h = jnp.maximum(h @ W_top1 + b_top1, 0.0)
    h = jnp.maximum(h @ W_top2 + b_top2, 0.0)
    y = h @ W_top3
    return y

_drawn_inputs = setup_inputs


def setup_inputs(seed=0):
    import zlib

    import numpy as np

    out = dict(_drawn_inputs(seed))
    spreads = {'b_top1': (0.0, 2.0),
     'b_top2': (0.0, 0.456),
     'L0_rec_b0': (0.0, 0.1),
     'L0_rec_b1': (0.0, 0.1)}
    factors = {'tbl_0': 8.0,
     'tbl_1': 8.0,
     'tbl_2': 8.0,
     'tbl_3': 8.0,
     'tbl_4': 8.0,
     'tbl_5': 8.0,
     'tbl_6': 8.0,
     'tbl_7': 8.0,
     'tbl_8': 8.0,
     'tbl_9': 8.0,
     'tbl_10': 8.0,
     'tbl_11': 8.0,
     'tbl_12': 8.0,
     'tbl_13': 8.0,
     'tbl_14': 8.0,
     'tbl_15': 8.0,
     'tbl_16': 8.0,
     'tbl_17': 8.0,
     'tbl_18': 8.0,
     'tbl_19': 8.0,
     'tbl_20': 8.0,
     'tbl_21': 8.0,
     'tbl_22': 8.0,
     'tbl_23': 8.0,
     'tbl_24': 8.0,
     'tbl_25': 8.0,
     'tbl_26': 8.0,
     'tbl_27': 8.0,
     'tbl_28': 8.0,
     'tbl_29': 8.0,
     'tbl_30': 8.0,
     'tbl_31': 8.0,
     'L0_rec_W0': 8.0,
     'L0_rec_W1': 3.619,
     'L0_rec_W2': 8.0,
     'dense_ctx': 3.653}
    for name, (base, spread) in spreads.items():
        noise = np.random.default_rng([zlib.crc32(name.encode()), seed]).standard_normal(out[name].shape)
        drawn = base * np.exp(spread * noise) if base else spread * noise
        out[name] = jnp.asarray(drawn.astype(out[name].dtype))
    for name, factor in factors.items():
        out[name] = (out[name] * factor).astype(out[name].dtype)
    return out
```

```python
import concourse.bass as bass
from concourse import mybir
from contextlib import ExitStack



def build(nc, dense_ctx, ids, tables, W_top1, b_top1, W_top2, b_top2, W_top3,
          W0, b0, W1, b1, W2, b2, out):
    f32 = mybir.dt.float32
    f32r = mybir.dt.float32r
    i32 = mybir.dt.int32
    ALU = mybir.AluOpType
    ACT = mybir.ActivationFunctionType

    BATCH, F = ids.shape
    D = tables[0].shape[1]
    ND = dense_ctx.shape[1]
    O = W0.shape[0]
    H = O // 2
    P = 128
    NBLK = BATCH // P
    DS = 8
    SPB = D // DS
    NSUP = NBLK * SPB
    W = DS * P
    HW = W // 2
    QW = W // 4
    NA, NC, NBJ = F // 8, F // 16, H // 16
    T1, T2 = W_top1.shape[1], W_top2.shape[1]
    M1, M2 = T1 // P, T2 // P

    L0 = [(0, 0), (0, 1), (1, 0), (1, 1), (2, 1), (3, 1)]
    L1 = [(i, j) for i in range(NA) for j in range(NBJ)]
    N0, N1 = len(L0), len(L1)
    STEP = N0 + N1
    NP = 8
    assert (SPB * STEP) % NP == 0
    GRP = 1 + 2 * (NC + NA) + 1
    assert GRP % 2 == 0
    AFTER = [N1 - GRP + q for q in range(GRP)]
    ROT = 2 * (NBJ - 1)

    ctx = ExitStack()
    with ctx:
        def sb(name, shape, dt=f32):
            return ctx.enter_context(nc.sbuf_tensor(name, shape, dt))

        def ps(name, shape):
            return ctx.enter_context(nc.psum_tensor(name, shape, f32))

        def sem(name):
            return ctx.enter_context(nc.semaphore(name))

        ids_all = sb("ids_all", [P, NBLK * F], i32)
        ids_cur = sb("ids_cur", [P, F], i32)
        dense_all = sb("dense_all", [P, NBLK * ND])
        e_gather = sb("e_gather", [P, F * D])
        e_work = sb("e_work", [P, 2 * F * D], f32r)
        dense_work = sb("dense_work", [P, ND])
        x2 = sb("x2", [P, HW], f32r)
        sel_a = sb("sel_a", [P, NA, P], f32r)
        sel_c = sb("sel_c", [P, NC, P], f32r)
        sel_q = sb("sel_q", [P, 2, P], f32r)
        xa = sb("xa", [P, 2, NA, W])
        xc = sb("xc", [P, 2, NC, W])
        xq = sb("xq", [P, 4, QW])
        hb = sb("hb", [P, 2, NBJ, W])
        prod = sb("prod", [P, NP, W])
        direct = sb("direct", [P, 2, W])
        z1h = sb("z1h", [P, W])
        v2 = sb("v2", [P, QW])
        r2 = sb("r2", [P, QW])
        acc = sb("acc", [P, W])
        acc2 = sb("acc2", [P, QW])
        zs = sb("zs", [P, BATCH])
        zsx = sb("zsx", [64, BATCH])
        w0t = sb("w0t", [P, N0, O])
        w1t = sb("w1t", [P, N1, O])
        w2t = sb("w2t", [P, F])
        wt1a = sb("wt1a", [P, T1])
        wt1b = sb("wt1b", [64, T1])
        wt2 = sb("wt2", [P, M1, T2])
        wt3 = sb("wt3", [P, M2])
        b0c = sb("b0c", [P, 1])
        b1c = sb("b1c", [P, 1])
        b2c = sb("b2c", [4, 1])
        bt1 = sb("bt1", [P, M1])
        bt2 = sb("bt2", [P, M2])
        ident = sb("ident", [P, P])
        sel4 = sb("sel4", [P, 4])
        stage = hb[:, :, :, :].rearrange("p a b c -> p (a b c)")
        w0s = stage[:, 0:F * F]
        w1s = stage[:, F * F:F * F + H * F]
        w1p = stage[:, F * F + H * F:F * F + 2 * H * F]
        w0p = stage[:, F * F + 2 * H * F:F * F + 2 * H * F + N0 * P]
        space = prod[:, :, :].rearrange("p a b -> p (a b)")
        h1 = space[:, 0:M1 * HW].rearrange("p (m c) -> p m c", m=M1)
        h2 = space[:, M1 * HW:(M1 + M2) * HW].rearrange("p (m c) -> p m c", m=M2)
        y = space[0:1, (M1 + M2) * HW:(M1 + M2) * HW + BATCH]

        Z0 = ps("Z0", [P, W])
        Z1 = ps("Z1", [P, W])
        TP = ps("TP", [P, 2 * HW])
        G = ps("G", [P, HW])
        S = ps("S", [P, HW])

        ids_in = sem("ids_in")
        w_in = sem("w_in")
        small_in = sem("small_in")
        const_ready = sem("const_ready")
        pool_step = sem("pool_step")
        gathered = sem("gathered")
        pool_held = sem("pool_held")
        pe_held = sem("pe_held")
        e_ready = sem("e_ready")
        w_arranged = sem("w_arranged")
        sel_ready = sem("sel_ready")
        w_turned = sem("w_turned")
        w_ready = sem("w_ready")
        t_done = sem("t_done")
        t_evac = sem("t_evac")
        dense_ready = sem("dense_ready")
        prod_done = sem("prod_done")
        tile_used = sem("tile_used")
        h_ready = sem("h_ready")
        d0_ready = sem("d0_ready")
        d0_free = sem("d0_free")
        b_rot = [sem("b_rot0"), sem("b_rot1")]
        z1h_ready = sem("z1h_ready")
        d1_ready = sem("d1_ready")
        d1_free = sem("d1_free")
        g_done = sem("g_done")
        v_done = sem("v_done")
        s_done = sem("s_done")
        r_ready = sem("r_ready")
        r_free = sem("r_free")
        zs_ready = sem("zs_ready")
        top1_done = sem("top1_done")
        h1_ready = sem("h1_ready")
        top2_done = sem("top2_done")
        h2_ready = sem("h2_ready")
        top3_done = sem("top3_done")
        y_ready = sem("y_ready")
        y_out = sem("y_out")

        def before(n, s, last):
            return n * (SPB * STEP) + 2 * N0 + s * STEP - (N0 if last and s == SPB - 1 else 0)

        def slot_of(s, last, k):
            return (2 * N0 + s * STEP - (N0 if last and s == SPB - 1 else 0) + k) % NP

        def more(s, last):
            return not (last and s + 2 >= SPB)

        block = ctx.enter_context(nc.Block())

        @block.sync
        def _(sp):
            sp.dma_start(ids_all[:, :].rearrange("p (n f) -> p n f", f=F),
                         ids.rearrange("(n p) f -> p n f", p=P)).then_inc(ids_in, 16)
            sp.dma_start(w0s, W0).then_inc(w_in, 16)
            sp.dma_start(w1s[0:H, :], W1[H:O, :]).then_inc(w_in, 16)
            sp.dma_start(w1s[H:O, :], W1[0:H, :]).then_inc(w_in, 16)
            loads = [
                (dense_all[:, :].rearrange("p (n f) -> p n f", f=ND),
                 dense_ctx.rearrange("(n p) f -> p n f", p=P)),
                (b0c[:, :], b0.rearrange("(p a) -> p a", a=1)),
                (b1c[0:H, :], b1[H:O].rearrange("(p a) -> p a", a=1)),
                (b1c[H:O, :], b1[0:H].rearrange("(p a) -> p a", a=1)),
                (b2c[:, :], b2.rearrange("(p a) -> p a", a=1).to_broadcast([4, 1])),
                (w2t[H:O, :], W2.rearrange("a (h m) -> (a h) m", m=F)),
                (wt1a[0:H, :], W_top1[H:2 * H, :]),
                (wt1a[H:O, :], W_top1[0:H, :]),
                (wt2[:, :, :], W_top2.rearrange("(k p) n -> p k n", p=P)),
                (wt3[:, :], W_top3.rearrange("(k p) a -> p (k a)", p=P)),
                (bt1[:, :], b_top1.rearrange("(k p) -> p k", p=P)),
                (bt2[:, :], b_top2.rearrange("(k p) -> p k", p=P)),
            ]
            for dst, src in loads:
                sp.dma_start(dst, src, allow_slow_non_contiguous=dst.shape[-1] < 8)\
                    .then_inc(small_in, 16)
            sp.wait_ge(const_ready, 1)
            sp.dma_start(wt1b[0:ND, :], W_top1[2 * H + 1:2 * H + 1 + ND, :]).then_inc(small_in, 16)
            sp.dma_start(wt1b[32:36, :], W_top1[2 * H:2 * H + 1, :].to_broadcast([4, T1])).then_inc(small_in, 16)
            with sp.Fori(0, NSUP // 2) as pair:
                for slot in range(2):
                    sp.wait_ge(h_ready, pair * 4 + (2 * slot + 2))
                    for j in range(1, NBJ):
                        sp.dma_start(hb[0:P - 16 * j, slot, j, :], hb[16 * j:P, slot, 0, :])\
                            .then_inc(b_rot[slot], 16)
                        sp.dma_start(hb[P - 16 * j:P, slot, j, :], hb[0:16 * j, slot, 0, :])\
                            .then_inc(b_rot[slot], 16)
            sp.wait_ge(y_ready, BATCH // HW)
            sp.dma_start(out.rearrange("b a -> a b"), y).then_inc(y_out, 16)
            sp.wait_ge(y_out, 16)
        NSMALL = 14 * 16
        READY = SPB + 1

        @block.gpsimd
        def _(pool):
            pool.sem_inc(d0_free, 2)
            pool.sem_inc(d1_free, 2)
            pool.sem_inc(r_free, 1)

            def held():
                pool.sem_inc(pool_held, 1)

            def gather(m, fields):
                held()
                for f in fields:
                    nc.gpsimd.indirect_dma_start(
                        e_gather[:, f * D:(f + 1) * D], None, tables[f],
                        bass.IndirectOffsetOnAxis(ids_cur[:, f:f + 1], 0)).then_inc(gathered, 16)
                pool.wait_ge(gathered, m * (16 * F) + 16 * (fields[-1] + 1))

            nc.gpsimd.memset(wt1b[:, :], 0.0).then_inc(const_ready, 1)
            pool.wait_ge(ids_in, 16)
            nc.gpsimd.tensor_copy(ids_cur[:, :], ids_all[:, 0:F]).then_inc(pool_step, 1)
            pool.wait_ge(pool_step, 1)
            gather(0, range(F))
            nc.gpsimd.memset(ident[:, :], 0.0).then_inc(pool_step, 1)
            pool.wait_ge(pool_step, 2)
            nc.gpsimd.affine_select(out=ident[:, :], in_=ident[:, :], compare_op=ALU.not_equal,
                                    fill=1.0, base=0, pattern=[[-1, P]], channel_multiplier=1)\
                .then_inc(const_ready, 1)
            nc.gpsimd.memset(zsx[:, :], 0.0).then_inc(const_ready, 1)
            nc.gpsimd.memset(sel4[:, :], 0.0).then_inc(pool_step, 1)
            pool.wait_ge(pool_step, 3)
            for q in range(4):
                nc.gpsimd.memset(sel4[32 * q:32 * q + 32, q:q + 1], 1.0).then_inc(const_ready, 1)
            eg = e_gather[:, :].rearrange("p (f s h e) -> p s h e f", s=SPB, h=2, e=4)
            ew = e_work[:, :].rearrange("p (s e h t f) -> p s h e t f", s=SPB, h=2, e=4, t=2)

            def split(m, at):
                for sup in range(SPB):
                    nc.gpsimd.tensor_copy(ew[:, sup, :, :, 0, :], eg[:, sup, :, :, :])\
                        .then_inc(pool_step, 1)
                at += SPB
                pool.wait_ge(pool_step, at)
                for sup in range(SPB):
                    nc.gpsimd.tensor_tensor(ew[:, sup, :, :, 1, :], eg[:, sup, :, :, :],
                                            ew[:, sup, :, :, 0, :].bitcast(f32), ALU.subtract)\
                        .then_inc(e_ready, 1)
                nc.gpsimd.tensor_copy(dense_work[:, :], dense_all[:, bass.ds(m * ND, ND)])\
                    .then_inc(e_ready, 1)
                pool.wait_ge(e_ready, m * READY + READY)
                return at

            def fetch_ids(m, at):
                nc.gpsimd.tensor_copy(ids_cur[:, :], ids_all[:, bass.ds(m * F, F)])\
                    .then_inc(pool_step, 1)
                at += 1
                pool.wait_ge(pool_step, at)
                return at

            pool.wait_ge(const_ready, 7)
            pool.wait_ge(small_in, NSMALL)
            at = fetch_ids(1, split(0, 3))
            gather(1, range(F))

            BEGUN = at
            lo, hi = slice(0, H), slice(H, O)

            def add_direct(half, m, s):
                ready, free = ((d0_ready, d0_free), (d1_ready, d1_free))[half]
                rows = hi if half == 0 else lo
                src = direct[rows, s % 2, :]
                pool.wait_ge(ready, m * SPB + (s + 1))
                if s == 0:
                    held()
                    nc.gpsimd.tensor_copy(acc[rows, :], src).then_inc(free, 1)
                else:
                    nc.gpsimd.tensor_tensor(acc[rows, :], acc[rows, :], src, ALU.add)\
                        .then_inc(free, 1)
                pool.wait_ge(free, m * SPB + (2 + s + 1))

            def fold(half, m, at):
                rows = hi if half == 0 else lo
                for w in (W // 2, W // 4):
                    nc.gpsimd.tensor_tensor(acc[rows, 0:w], acc[rows, 0:w], acc[rows, w:2 * w],
                                            ALU.add).then_inc(pool_step, 1)
                    at += 1
                    pool.wait_ge(pool_step, at)
                nc.gpsimd.tensor_tensor(zs[rows, bass.ds(m * P, P)], acc[rows, 0:P],
                                        acc[rows, P:2 * P], ALU.add).then_inc(zs_ready, 1)
                pool.wait_ge(zs_ready, m * 3 + (half + 1))
                return at

            def add_layer2(n, s):
                rows = slice(32, 36)
                pool.wait_ge(r_ready, n * SPB + (s + 1))
                if s == 0:
                    held()
                    nc.gpsimd.tensor_copy(acc2[rows, :], r2[rows, :]).then_inc(r_free, 1)
                else:
                    nc.gpsimd.tensor_tensor(acc2[rows, :], acc2[rows, :], r2[rows, :], ALU.add)\
                        .then_inc(r_free, 1)
                pool.wait_ge(r_free, n * SPB + (1 + s + 1))
                if s == SPB - 1:
                    nc.gpsimd.tensor_tensor(zsx[rows, bass.ds(n * P, P)], acc2[rows, 0:P],
                                            acc2[rows, P:2 * P], ALU.add).then_inc(zs_ready, 1)
                    pool.wait_ge(zs_ready, n * 3 + 3)

            BLOCK = 4 + SPB + 1
            SPREAD = {1: range(0, 8), 2: range(8, 20), 3: range(20, F)}

            def one_block(n, at, copy, fetch, last):
                for s in range(SPB):
                    add_direct(1, n, s)
                    if s == SPB - 1:
                        at = fold(1, n, at)
                    if more(s, last):
                        add_direct(0, n + (s + 2) // SPB, (s + 2) % SPB)
                        if s + 2 == SPB - 1:
                            at = fold(0, n, at)
                    add_layer2(n, s)
                    if s == 1 and copy:
                        pool.wait_ge(t_done, n * (SPB * GRP) + SPB * GRP)
                        held()
                        at = split(n + 1, at)
                    if s == 1 and fetch:
                        at = fetch_ids(n + 2, at)
                    if fetch and s in SPREAD:
                        gather(n + 2, SPREAD[s])
                return at

            add_direct(0, 0, 0)
            add_direct(0, 0, 1)
            with pool.Fori(0, NBLK - 2) as n:
                one_block(n, n * BLOCK + BEGUN, True, True, False)
            at = one_block(NBLK - 2, (NBLK - 2) * BLOCK + BEGUN, True, False, False)
            one_block(NBLK - 1, at, False, False, True)

        @block.scalar
        def _(act):
            def evac_t(slot, q, gi, n_dense):
                act.wait_ge(t_done, gi + (q + 1))
                src = TP[:, q % 2 * HW:(q % 2 + 1) * HW]
                half = slice((q + 1) % 2 * HW, ((q + 1) % 2 + 1) * HW)
                if q == 0:
                    dst = x2[:, :]
                elif q < 1 + 2 * NC:
                    dst = xc[:, slot % 2, (q - 1) // 2, half]
                elif q < GRP - 1:
                    dst = xa[:, slot % 2, (q - 1 - 2 * NC) // 2, half]
                else:
                    dst = xq[:, slot % 4, :]
                    if n_dense is not None:
                        nc.scalar.activation(zsx[0:ND, bass.ds(n_dense * P, P)],
                                             src[0:ND, QW:QW + P], ACT.Copy).then_inc(dense_ready, 1)
                    src = src[:, 0:QW]
                nc.scalar.activation(dst, src, ACT.Copy).then_inc(t_evac, 1)

            def evac_z0(slot, g, tiles):
                act.wait_ge(tile_used, tiles + NP)
                for part in range(2):
                    nc.scalar.activation(hb[part * H:(part + 1) * H, slot, 0, :], Z0[0:H, :], ACT.Relu,
                                         bias=b0c[0:H, :]).then_inc(h_ready, 1)
                act.wait_ge(d0_free, g + 1)
                nc.scalar.activation(direct[H:O, slot, :], Z0[H:O, :], ACT.Relu,
                                     bias=b0c[H:O, :]).then_inc(d0_ready, 1)

            act.wait_ge(small_in, NSMALL)
            act.wait_ge(const_ready, 7)
            for g in range(2):
                for q in range(GRP):
                    evac_t(g, q, g * GRP, 0 if g == 0 else None)
            for g in range(2):
                evac_z0(g, g, (g + 1) * N0)

            def one_block(n, last):
                for s in range(SPB):
                    g = n * SPB + s
                    if more(s, last):
                        for q in range(GRP):
                            i, half = divmod(q - 1 - 2 * NC, 2)
                            if 0 <= i < NA and half == 0:
                                act.wait_ge(prod_done, before(n, s, last) + NBJ * (i + 1))
                            evac_t((s + 2) % 4, q, n * (SPB * GRP) + (s + 2) * GRP,
                                   n + 1 if s + 2 == SPB else None)
                    act.wait_ge(tile_used, before(n, s, last) + (N1 + NP))
                    nc.scalar.activation(z1h[H:O, :], Z1[H:O, :], ACT.Relu,
                                         bias=b1c[H:O, :]).then_inc(z1h_ready, 1)
                    act.wait_ge(d1_free, g + 1)
                    nc.scalar.activation(direct[0:H, s % 2, :], Z1[0:H, :], ACT.Relu,
                                         bias=b1c[0:H, :]).then_inc(d1_ready, 1)
                    if more(s, last):
                        evac_z0(s % 2, n * SPB + (s + 2), before(n, s, last) + STEP)
                    act.wait_ge(s_done, g + 1)
                    act.wait_ge(r_free, g + 1)
                    nc.scalar.activation(r2[32:36, :], S[0:4, 0:QW], ACT.Relu,
                                         bias=b2c[:, :]).then_inc(r_ready, 1)

            with act.Fori(0, NBLK - 1) as n:
                one_block(n, False)
            one_block(NBLK - 1, True)

            with act.Fori(0, BATCH // HW) as c:
                for m in range(M1):
                    act.wait_ge(top1_done, c * M1 + (m + 1))
                    src = (Z0, Z1)[m // 2][:, m % 2 * HW:(m % 2 + 1) * HW]
                    nc.scalar.activation(h1[:, m, :], src, ACT.Relu, bias=bt1[:, m:m + 1])\
                        .then_inc(h1_ready, 1)
                for m in range(M2):
                    act.wait_ge(top2_done, c * M2 + (m + 1))
                    nc.scalar.activation(h2[:, m, :], TP[:, m * HW:(m + 1) * HW], ACT.Relu,
                                         bias=bt2[:, m:m + 1]).then_inc(h2_ready, 1)
                act.wait_ge(top3_done, c + 1)
                nc.scalar.activation(y[:, bass.ds(c * HW, HW)], G[0:1, :], ACT.Copy).then_inc(y_ready, 1)

        @block.vector
        def _(dve):
            dve.wait_ge(w_in, 3 * 16)
            w0v = w0s.rearrange("o (a b) -> o a b", b=F)
            for t, (i, j) in enumerate(L0):
                dst = w0p[:, t * P:(t + 1) * P].rearrange("o (u v) -> o u v", v=16)
                plain = w0v[:, 8 * i:8 * i + 8, 16 * j:16 * j + 16]
                if i < 2 and j == 1:
                    turned = w0v[:, 16:32, 8 * i:8 * i + 8].rearrange("o v u -> o u v")
                    nc.vector.tensor_tensor(dst, plain, turned, ALU.add).then_inc(w_arranged, 1)
                else:
                    nc.vector.tensor_copy(dst, plain).then_inc(w_arranged, 1)
            w1v = w1s.rearrange("o (h v i r k) -> o h i r k v", v=16, i=NA, r=2, k=4)
            w1pv = w1p.rearrange("o (i j r k v) -> o j i r k v", i=NA, j=NBJ, r=2, k=4)
            for j in range(NBJ):
                for k in range(4):
                    nc.vector.tensor_copy(w1pv[:, j, :, :, k, :], w1v[:, (k + j) % 4, :, :, k, :])\
                        .then_inc(w_arranged, 1)
            nc.vector.memset(sel_q[:, :, :].rearrange("p a b -> p (a b)").bitcast(f32), 0.0)\
                .then_inc(sel_ready, 1)
            dve.wait_ge(const_ready, 7)
            dve.wait_ge(sel_ready, 1)
            for r in range(4):
                rows, half = slice(32 * r, 32 * r + 32), r // 2
                square = ident[rows, rows]
                nc.vector.tensor_copy(
                    sel_a[rows, :, :].rearrange("p i (u v) -> p (i u) v", v=16),
                    square.unsqueeze(2).to_broadcast([32, F, 16])).then_inc(sel_ready, 1)
                for j in range(NC):
                    nc.vector.tensor_copy(
                        sel_c[rows, j, :].rearrange("p (u v) -> p u v", v=16),
                        ident[rows, 32 * r + 16 * j:32 * r + 16 * j + 16].unsqueeze(1)
                        .to_broadcast([32, 8, 16])).then_inc(sel_ready, 1)
                for k in range(2):
                    q = 2 * half + k
                    nc.vector.tensor_copy(sel_q[rows, k, 32 * q:32 * q + 32], square)\
                        .then_inc(sel_ready, 1)
            dve.wait_ge(w_turned, 1)
            nc.vector.tensor_copy(w0t[:, :, :].rearrange("p t o -> p (t o)"), Z0[:, 0:N0 * O])\
                .then_inc(w_ready, 1)
            dve.wait_ge(w_turned, 2)
            w1f = w1t[:, :, :].rearrange("p t o -> p (t o)")
            nc.vector.tensor_copy(w1f[:, 0:W], Z1[:, :]).then_inc(w_ready, 1)
            nc.vector.tensor_copy(w1f[:, W:2 * W], TP[:, :]).then_inc(w_ready, 1)

            def layer0(slot, idx, slot0, groups):
                done = -1
                for t, (i, j) in enumerate(L0):
                    need = 1 + 2 * NC + 2 * (i + 1)
                    if need > done:
                        dve.wait_ge(t_evac, groups + need)
                        done = need
                    dve.wait_ge(tile_used, idx + (t + 1))
                    nc.vector.tensor_tensor(prod[:, (slot0 + t) % NP, :], xa[:, slot % 2, i, :],
                                            xc[:, slot % 2, j, :], ALU.mult).then_inc(prod_done, 1)

            for g in range(2):
                layer0(g, g * N0, g * N0, g * GRP)

            def one_block(n, last):
                for s in range(SPB):
                    base, slot0 = before(n, s, last), slot_of(s, last, 0)
                    dve.wait_ge(b_rot[s % 2], n * (16 * ROT * SPB // 2) + 16 * ROT * (s // 2 + 1))
                    for t, (i, j) in enumerate(L1):
                        dve.wait_ge(tile_used, base + (t + 1))
                        nc.vector.tensor_tensor(prod[:, (slot0 + t) % NP, :], xa[:, s % 2, i, :],
                                                hb[:, s % 2, j, :], ALU.mult).then_inc(prod_done, 1)
                    if more(s, last):
                        layer0(s, base + N1, slot0 + N1, n * (SPB * GRP) + (s + 2) * GRP)
                    dve.wait_ge(g_done, n * SPB + (s + 1))
                    dve.wait_ge(s_done, n * SPB + s)
                    nc.vector.tensor_tensor(v2[:, :], G[:, 0:QW], xq[:, s, :], ALU.mult)\
                        .then_inc(v_done, 1)

            with dve.Fori(0, NBLK - 1) as n:
                one_block(n, False)
            one_block(NBLK - 1, True)

        @block.tensor
        def _(pe):
            pe.sem_inc(tile_used, NP)
            pe.wait_ge(const_ready, 7)
            pe.wait_ge(w_arranged, N0 + 4 * NBJ)
            for t in range(N0):
                last = nc.tensor.transpose(Z0[:, t * O:(t + 1) * O], w0p[:, t * P:(t + 1) * P],
                                           ident[:, :])
            last.then_inc(w_turned, 1)
            for t in range(N1):
                bank = (Z1, TP)[t // 8]
                last = nc.tensor.transpose(bank[:, t % 8 * O:(t % 8 + 1) * O], w1p[:, t * P:(t + 1) * P],
                                           ident[:, :])
            last.then_inc(w_turned, 1)

            def turn(s, q):
                bank = TP[:, q % 2 * HW:(q % 2 + 1) * HW]
                if q == 0:
                    for e in range(4):
                        cols = slice((s * 4 + e) * P, (s * 4 + e + 1) * P)
                        last = nc.tensor.transpose(bank[:, e * P:(e + 1) * P],
                                                   e_work[:, cols].bitcast(f32), ident[:, :])
                elif q < GRP - 1:
                    k, half = divmod(q - 1, 2)
                    rows = slice(64 * half, 64 * half + 64)
                    sel = sel_c[rows, k, :] if k < NC else sel_a[rows, k - NC, :]
                    last = nc.tensor.matmul(bank, sel, x2[rows, :], start=True, stop=True)
                else:
                    if s == 0:
                        nc.tensor.transpose(bank[0:ND, QW:QW + P], dense_work[:, :], ident[:, :])
                    for k in range(2):
                        last = nc.tensor.matmul(bank[:, 0:QW], sel_q[:, k, :], x2[:, k * QW:(k + 1) * QW],
                                                start=(k == 0), stop=(k == 1))
                last.then_inc(t_done, 1)

            def tile(Z, wt, t, count, slot, idx):
                pe.wait_ge(prod_done, idx)
                for b in range(2):
                    last = nc.tensor.matmul(Z[:, b * HW:(b + 1) * HW], wt[:, t, :],
                                            prod[:, slot % NP, b * HW:(b + 1) * HW],
                                            start=(t == 0), stop=(t == count - 1))
                last.then_inc(tile_used, 1)
                return last

            pe.wait_ge(w_ready, 3)
            pe.wait_ge(sel_ready, 1 + 4 * (1 + NC + 2))
            pe.wait_ge(e_ready, READY)
            for g in range(2):
                for q in range(GRP):
                    if g * GRP + q:
                        pe.wait_ge(t_evac, g * GRP + max(q - 1, 1 if q else 0))
                    turn(g, q)
            for g in range(2):
                if g:
                    pe.wait_ge(d0_ready, g)
                for t in range(N0):
                    tile(Z0, w0t, t, N0, g * N0 + t, g * N0 + t + 1)

            def layer2_products(n, s):
                pe.wait_ge(z1h_ready, n * SPB + (s + 1))
                pe.wait_ge(v_done, n * SPB + s)
                pe.sem_inc(pe_held, 1)
                for q in range(4):
                    last = nc.tensor.matmul(G[32 * q:32 * q + 32, 0:QW], w2t[H:O, :],
                                            z1h[H:O, q * QW:(q + 1) * QW], start=True, stop=True)
                last.then_inc(g_done, 1)

            def one_block(n, last):
                for s in range(SPB):
                    base, slot0 = before(n, s, last), slot_of(s, last, 0)
                    pe.wait_ge(d1_ready, n * SPB + s)
                    for t in range(N1):
                        tile(Z1, w1t, t, N1, slot0 + t, base + (t + 1))
                        if t in AFTER and more(s, last):
                            q = AFTER.index(t)
                            if q == 0 and s + 2 == SPB:
                                pe.wait_ge(e_ready, n * READY + 2 * READY)
                            pe.wait_ge(t_evac, n * (SPB * GRP) + (s + 2) * GRP + (1 if q == 1 else q - 1))
                            turn((s + 2) % SPB, q)
                    if more(s, last):
                        pe.wait_ge(d0_ready, n * SPB + (s + 2))
                        for t in range(N0):
                            if t == N0 // 2:
                                layer2_products(n, s)
                            tile(Z0, w0t, t, N0, slot0 + N1 + t, base + (N1 + t + 1))
                    else:
                        layer2_products(n, s)
                    pe.wait_ge(v_done, n * SPB + (s + 1))
                    pe.wait_ge(r_ready, n * SPB + s)
                    nc.tensor.matmul(S[0:4, 0:QW], sel4[:, :], v2[:, :], start=True, stop=True)\
                        .then_inc(s_done, 1)

            with pe.Fori(0, NBLK - 1) as n:
                one_block(n, False)
            one_block(NBLK - 1, True)

            pe.wait_ge(zs_ready, 3 * NBLK)
            pe.wait_ge(dense_ready, NBLK)
            pe.wait_ge(d1_ready, NSUP)
            with pe.Fori(0, BATCH // HW) as c:
                pe.wait_ge(h1_ready, c * M1)
                for m in range(M1):
                    dst = (Z0, Z1)[m // 2][:, m % 2 * HW:(m % 2 + 1) * HW]
                    nc.tensor.matmul(dst, wt1a[:, m * P:(m + 1) * P], zs[:, bass.ds(c * HW, HW)],
                                     start=True, stop=False)
                    nc.tensor.matmul(dst, wt1b[:, m * P:(m + 1) * P], zsx[:, bass.ds(c * HW, HW)],
                                     start=False, stop=True).then_inc(top1_done, 1)
                for k in range(M1):
                    pe.wait_ge(h1_ready, c * M1 + (k + 1))
                    for m in range(M2):
                        last = nc.tensor.matmul(TP[:, m * HW:(m + 1) * HW], wt2[:, k, m * P:(m + 1) * P],
                                                h1[:, k, :], start=(k == 0), stop=(k == M1 - 1))
                        if k == M1 - 1:
                            last.then_inc(top2_done, 1)
                for k in range(M2):
                    pe.wait_ge(h2_ready, c * M2 + (k + 1))
                    last = nc.tensor.matmul(G[0:1, :], wt3[:, k:k + 1], h2[:, k, :],
                                            start=(k == 0), stop=(k == M2 - 1))
                last.then_inc(top3_done, 1)


_INS = (["dense_ctx", "ids"] + [f"tbl_{f}" for f in range(32)]
        + ["W_top1", "b_top1", "W_top2", "b_top2", "W_top3"]
        + [f"L0_rec_{w}" for w in ("W0", "b0", "W1", "b1", "W2", "b2")])


def kernel(**inputs):
    import numpy as _np
    import concourse.bacc as _bacc
    from concourse import mybir as _mybir
    from concourse.bass_utils import run_bass_kernel_spmd as _run

    nc = _bacc.Bacc("TRN2", target_bir_lowering=False, num_devices=1)
    arrays, aps = {}, {}
    for name in _INS:
        a = _np.ascontiguousarray(inputs[name])
        arrays[f"in_{name}"] = a
        aps[name] = nc.dram_tensor(f"in_{name}", a.shape, _mybir.dt.from_np(a.dtype), kind="ExternalInput").ap()
    batch = inputs["ids"].shape[0]
    out = nc.dram_tensor("out_y", (batch, 1), _mybir.dt.float32, kind="ExternalOutput").ap()
    build(nc, aps["dense_ctx"], aps["ids"], [aps[f"tbl_{f}"] for f in range(32)],
          *[aps[name] for name in _INS[34:]], out)
    r = _run(nc, [arrays], core_ids=[0])
    return r.results[0]["out_y"]
```

```python
import concourse.bass as bass
from concourse import mybir
from contextlib import ExitStack



def build(nc, dense_ctx, ids, tables, W_top1, b_top1, W_top2, b_top2, W_top3,
          W0, b0, W1, b1, W2, b2, out):
    f32 = mybir.dt.float32
    f32r = mybir.dt.float32r
    i32 = mybir.dt.int32
    ALU = mybir.AluOpType
    ACT = mybir.ActivationFunctionType
    AX = mybir.AxisListType

    BATCH, F = ids.shape
    D = tables[0].shape[1]
    ND = dense_ctx.shape[1]
    O = W0.shape[0]
    H = O // 2
    P = 128
    NBLK = BATCH // P
    DS = 8
    SPB = D // DS
    NSUP = NBLK * SPB
    W = DS * P
    HW = W // 2
    QW = W // 4
    NA, NC, NBJ = F // 8, F // 16, H // 16
    T1, T2 = W_top1.shape[1], W_top2.shape[1]
    M1, M2 = T1 // P, T2 // P

    ARR = [("v", 0, 1), ("v", 2, 3), ("u", 1, 3), ("v", 1, 3)] + [("u", i, i) for i in range(NA)]
    NS = len(ARR) - NA
    L0 = [(2, 3), (NS, 0), (NS, 1), (NS + 1, 1), (NS + 2, 1)]
    L1 = [(i, j) for i in range(NA) for j in range(NBJ)]
    N0, N1 = len(L0), len(L1)
    STEP = N1 + N0
    PLAIN, CUT = 0, 1
    KIND = [CUT if p % 2 else PLAIN for p in range(N1)] + [PLAIN, PLAIN, CUT, PLAIN, PLAIN]
    RING = [3, 3]
    NRAW = 2
    assert all(SPB * KIND.count(k) % RING[k] == 0 for k in (PLAIN, CUT))
    assert SPB * KIND.count(CUT) % NRAW == 0
    GRP = 1 + 2 * len(ARR) + 1
    assert GRP % 2 == 0
    PE_IN, DVE_IN, HI_IN = 5, 7, 7
    AFTER = {PE_IN: [0]} | {PE_IN + 1 + i: [1 + 2 * i, 2 + 2 * i] for i in range(len(ARR))}
    AFTER[max(AFTER) + 1] = [GRP - 1]
    assert max(AFTER) < N1
    ROT = 2 * (NBJ - 1)

    ctx = ExitStack()
    with ctx:
        def sb(name, shape, dt=f32):
            return ctx.enter_context(nc.sbuf_tensor(name, shape, dt))

        def ps(name, shape):
            return ctx.enter_context(nc.psum_tensor(name, shape, f32))

        def sem(name):
            return ctx.enter_context(nc.semaphore(name))

        ids_all = sb("ids_all", [P, NBLK * F], i32)
        ids_cur = sb("ids_cur", [P, F], i32)
        dense_all = sb("dense_all", [P, NBLK * ND])
        e_gather = sb("e_gather", [P, F * D])
        e_work = sb("e_work", [P, 2 * F * D], f32r)
        dense_work = sb("dense_work", [P, ND])
        x2 = sb("x2", [P, HW], f32r)
        sel = sb("sel", [P, len(ARR), P], f32r)
        sel_q = sb("sel_q", [P, 2, P], f32r)
        xs = sb("xs", [P, NS, W])
        xa = sb("xa", [P, 2, NA, W])
        xq = sb("xq", [P, 4, QW])
        hb = sb("hb", [P, 2, NBJ, W])
        plain = sb("plain", [P, RING[PLAIN], W])
        raw = sb("raw", [P, NRAW, W])
        high = sb("high", [P, RING[CUT], W], f32r)
        low = sb("low", [P, RING[CUT], W], f32r)
        direct = sb("direct", [P, W])
        dsum = sb("dsum", [P, 2, P])
        z1h = sb("z1h", [P, W])
        v2 = sb("v2", [P, QW])
        r2 = sb("r2", [P, QW])
        acc2 = sb("acc2", [P, QW])
        zs = sb("zs", [P, BATCH])
        zsx = sb("zsx", [64, BATCH])
        NPL, NCU = KIND.count(PLAIN), KIND.count(CUT)
        w_plain = sb("w_plain", [P, NPL, O])
        w_high = sb("w_high", [P, NCU, O], f32r)
        w_low = sb("w_low", [P, NCU, O], f32r)
        w2t = sb("w2t", [P, F])
        wt1a = sb("wt1a", [P, T1])
        wt1b = sb("wt1b", [64, T1])
        wt2 = sb("wt2", [P, M1, T2])
        wt3 = sb("wt3", [P, M2])
        b0c = sb("b0c", [P, 1])
        b1c = sb("b1c", [P, 1])
        b2c = sb("b2c", [4, 1])
        bt1 = sb("bt1", [P, M1])
        bt2 = sb("bt2", [P, M2])
        ident = sb("ident", [P, P])
        sel4 = sb("sel4", [P, 4])
        stage = hb[:, :, :, :].rearrange("p a b c -> p (a b c)")
        w0s = stage[:, 0:F * F]
        w1s = stage[:, F * F:F * F + H * F]
        w1p = stage[:, F * F + H * F:F * F + 2 * H * F]
        w0p = stage[:, F * F + 2 * H * F:F * F + 2 * H * F + N0 * P]
        h1 = stage[:, 0:M1 * HW].rearrange("p (m c) -> p m c", m=M1)
        h2 = stage[:, M1 * HW:(M1 + M2) * HW].rearrange("p (m c) -> p m c", m=M2)
        y = stage[0:1, (M1 + M2) * HW:(M1 + M2) * HW + BATCH]

        Z0 = ps("Z0", [P, W])
        Z1 = ps("Z1", [P, W])
        TP = ps("TP", [P, 2 * HW])
        G = ps("G", [P, HW])
        S = ps("S", [P, HW])

        ids_in = sem("ids_in")
        w_in = sem("w_in")
        small_in = sem("small_in")
        const_ready = sem("const_ready")
        pool_step = sem("pool_step")
        gathered = sem("gathered")
        pool_held = sem("pool_held")
        pe_held = sem("pe_held")
        e_ready = sem("e_ready")
        w_arranged = sem("w_arranged")
        sel_ready = sem("sel_ready")
        w_turned = sem("w_turned")
        w_cut = sem("w_cut")
        w_ready = sem("w_ready")
        t_done = sem("t_done")
        t_evac = sem("t_evac")
        dense_ready = sem("dense_ready")
        plain_done = sem("plain_done")
        raw_done = sem("raw_done")
        high_done = sem("high_done")
        low_done = sem("low_done")
        used = [sem("plain_used"), sem("cut_used")]
        h_ready = sem("h_ready")
        d0_ready = sem("d0_ready")
        b_rot = [sem("b_rot0"), sem("b_rot1")]
        z1h_ready = sem("z1h_ready")
        d1_ready = sem("d1_ready")
        summed = sem("summed")
        zs_low = sem("zs_low")
        zs_high = sem("zs_high")
        g_done = sem("g_done")
        v_done = sem("v_done")
        s_done = sem("s_done")
        r_ready = sem("r_ready")
        r_free = sem("r_free")
        zs_ready = sem("zs_ready")
        top1_done = sem("top1_done")
        h1_ready = sem("h1_ready")
        top2_done = sem("top2_done")
        h2_ready = sem("h2_ready")
        top3_done = sem("top3_done")
        y_ready = sem("y_ready")
        y_out = sem("y_out")

        def count(kind, n, s, last, p):
            return n * (SPB * KIND.count(kind)) + fixed(kind, s, last, p)

        def fixed(kind, s, last, p):
            l0 = KIND[N1:].count(kind)
            return 2 * l0 + s * KIND.count(kind) + KIND[:p].count(kind) \
                - (l0 if last and s == SPB - 1 else 0)

        def window(s, last, into):
            yield from ((s, p) for p in range(into, STEP if more(s, last) else N1))
            if not (last and s == SPB - 1):
                yield from ((s + 1, p) for p in range(into))

        def more(s, last):
            return not (last and s + 2 >= SPB)

        block = ctx.enter_context(nc.Block())

        @block.sync
        def _(sp):
            sp.dma_start(ids_all[:, :].rearrange("p (n f) -> p n f", f=F),
                         ids.rearrange("(n p) f -> p n f", p=P)).then_inc(ids_in, 16)
            sp.dma_start(w0s, W0).then_inc(w_in, 16)
            sp.dma_start(w1s[0:H, :], W1[H:O, :]).then_inc(w_in, 16)
            sp.dma_start(w1s[H:O, :], W1[0:H, :]).then_inc(w_in, 16)
            loads = [
                (dense_all[:, :].rearrange("p (n f) -> p n f", f=ND),
                 dense_ctx.rearrange("(n p) f -> p n f", p=P)),
                (b0c[:, :], b0.rearrange("(p a) -> p a", a=1)),
                (b1c[0:H, :], b1[H:O].rearrange("(p a) -> p a", a=1)),
                (b1c[H:O, :], b1[0:H].rearrange("(p a) -> p a", a=1)),
                (b2c[:, :], b2.rearrange("(p a) -> p a", a=1).to_broadcast([4, 1])),
                (w2t[H:O, :], W2.rearrange("a (h m) -> (a h) m", m=F)),
                (wt1a[0:H, :], W_top1[H:2 * H, :]),
                (wt1a[H:O, :], W_top1[0:H, :]),
                (wt2[:, :, :], W_top2.rearrange("(k p) n -> p k n", p=P)),
                (wt3[:, :], W_top3.rearrange("(k p) a -> p (k a)", p=P)),
                (bt1[:, :], b_top1.rearrange("(k p) -> p k", p=P)),
                (bt2[:, :], b_top2.rearrange("(k p) -> p k", p=P)),
            ]
            for dst, src in loads:
                sp.dma_start(dst, src, allow_slow_non_contiguous=dst.shape[-1] < 8)\
                    .then_inc(small_in, 16)
            sp.wait_ge(const_ready, 1)
            sp.dma_start(wt1b[0:ND, :], W_top1[2 * H + 1:2 * H + 1 + ND, :]).then_inc(small_in, 16)
            sp.dma_start(wt1b[32:36, :], W_top1[2 * H:2 * H + 1, :].to_broadcast([4, T1])).then_inc(small_in, 16)
            with sp.Fori(0, NSUP // 2) as pair:
                for slot in range(2):
                    sp.wait_ge(h_ready, pair * 4 + (2 * slot + 2))
                    for j in range(1, NBJ):
                        sp.dma_start(hb[0:P - 16 * j, slot, j, :], hb[16 * j:P, slot, 0, :])\
                            .then_inc(b_rot[slot], 16)
                        sp.dma_start(hb[P - 16 * j:P, slot, j, :], hb[0:16 * j, slot, 0, :])\
                            .then_inc(b_rot[slot], 16)
            sp.wait_ge(y_ready, BATCH // HW)
            sp.dma_start(out.rearrange("b a -> a b"), y).then_inc(y_out, 16)
            sp.wait_ge(y_out, 16)
        NSMALL = 14 * 16
        READY = SPB + 1

        @block.gpsimd
        def _(pool):
            pool.sem_inc(r_free, 1)

            def held():
                pool.sem_inc(pool_held, 1)

            def gather(m, fields):
                held()
                for f in fields:
                    nc.gpsimd.indirect_dma_start(
                        e_gather[:, f * D:(f + 1) * D], None, tables[f],
                        bass.IndirectOffsetOnAxis(ids_cur[:, f:f + 1], 0)).then_inc(gathered, 16)
                pool.wait_ge(gathered, m * (16 * F) + 16 * (fields[-1] + 1))

            nc.gpsimd.memset(wt1b[:, :], 0.0).then_inc(const_ready, 1)
            pool.wait_ge(ids_in, 16)
            nc.gpsimd.tensor_copy(ids_cur[:, :], ids_all[:, 0:F]).then_inc(pool_step, 1)
            pool.wait_ge(pool_step, 1)
            gather(0, range(F))
            nc.gpsimd.memset(ident[:, :], 0.0).then_inc(pool_step, 1)
            pool.wait_ge(pool_step, 2)
            nc.gpsimd.affine_select(out=ident[:, :], in_=ident[:, :], compare_op=ALU.not_equal,
                                    fill=1.0, base=0, pattern=[[-1, P]], channel_multiplier=1)\
                .then_inc(const_ready, 1)
            nc.gpsimd.memset(zsx[:, :], 0.0).then_inc(const_ready, 1)
            nc.gpsimd.memset(sel4[:, :], 0.0).then_inc(pool_step, 1)
            pool.wait_ge(pool_step, 3)
            for q in range(4):
                nc.gpsimd.memset(sel4[32 * q:32 * q + 32, q:q + 1], 1.0).then_inc(const_ready, 1)
            eg = e_gather[:, :].rearrange("p (f s h e) -> p s h e f", s=SPB, h=2, e=4)
            ew = e_work[:, :].rearrange("p (s e h t f) -> p s h e t f", s=SPB, h=2, e=4, t=2)

            def split(m, at):
                for sup in range(SPB):
                    nc.gpsimd.tensor_copy(ew[:, sup, :, :, 0, :], eg[:, sup, :, :, :])\
                        .then_inc(pool_step, 1)
                at += SPB
                pool.wait_ge(pool_step, at)
                for sup in range(SPB):
                    nc.gpsimd.tensor_tensor(ew[:, sup, :, :, 1, :], eg[:, sup, :, :, :],
                                            ew[:, sup, :, :, 0, :].bitcast(f32), ALU.subtract)\
                        .then_inc(e_ready, 1)
                nc.gpsimd.tensor_copy(dense_work[:, :], dense_all[:, bass.ds(m * ND, ND)])\
                    .then_inc(e_ready, 1)
                pool.wait_ge(e_ready, m * READY + READY)
                return at

            def fetch_ids(m, at):
                nc.gpsimd.tensor_copy(ids_cur[:, :], ids_all[:, bass.ds(m * F, F)])\
                    .then_inc(pool_step, 1)
                at += 1
                pool.wait_ge(pool_step, at)
                return at

            pool.wait_ge(const_ready, 7)
            pool.wait_ge(small_in, NSMALL)
            at = fetch_ids(1, split(0, 3))
            gather(1, range(F))

            BEGUN = at
            lo, hi = slice(0, H), slice(H, O)

            def add_direct(rows, count, slot, m, s):
                dst, src = zs[rows, bass.ds(m * P, P)], dsum[rows, slot, :]
                held()
                if s == 0:
                    nc.gpsimd.tensor_copy(dst, src).then_inc(count, 1)
                else:
                    nc.gpsimd.tensor_tensor(dst, dst, src, ALU.add).then_inc(count, 1)
                pool.wait_ge(count, m * SPB + (s + 1))

            def add_both(n, s, last):
                pool.wait_ge(summed, n * SPB + (s + 3))
                add_direct(lo, zs_low, s % 2, n, s)
                if more(s, last):
                    add_direct(hi, zs_high, s % 2, n + (s + 2) // SPB, (s + 2) % SPB)

            def add_layer2(n, s):
                rows = slice(32, 36)
                pool.wait_ge(r_ready, n * SPB + (s + 1))
                if s == 0:
                    held()
                    nc.gpsimd.tensor_copy(acc2[rows, :], r2[rows, :]).then_inc(r_free, 1)
                else:
                    nc.gpsimd.tensor_tensor(acc2[rows, :], acc2[rows, :], r2[rows, :], ALU.add)\
                        .then_inc(r_free, 1)
                pool.wait_ge(r_free, n * SPB + (1 + s + 1))
                if s == SPB - 1:
                    held()
                    nc.gpsimd.tensor_tensor(zsx[rows, bass.ds(n * P, P)], acc2[rows, 0:P],
                                            acc2[rows, P:2 * P], ALU.add).then_inc(zs_ready, 1)
                    pool.wait_ge(zs_ready, n + 1)

            BLOCK = SPB + 1
            SPREAD = {1: range(0, 8), 2: range(8, 20), 3: range(20, F)}

            def one_block(n, at, copy, fetch, last):
                for s in range(SPB):
                    if s == 1 and copy:
                        pool.wait_ge(t_done, n * (SPB * GRP) + ((SPB - 1) * GRP + 1))
                        held()
                        at = split(n + 1, at)
                    if s == 1 and fetch:
                        at = fetch_ids(n + 2, at)
                    if fetch and s in SPREAD:
                        gather(n + 2, SPREAD[s])
                    add_both(n, s, last)
                    add_layer2(n, s)
                return at

            for g in range(2):
                pool.wait_ge(summed, g + 1)
                add_direct(hi, zs_high, g, 0, g)
            with pool.Fori(0, NBLK - 2) as n:
                one_block(n, n * BLOCK + BEGUN, True, True, False)
            at = one_block(NBLK - 2, (NBLK - 2) * BLOCK + BEGUN, True, False, False)
            one_block(NBLK - 1, at, False, False, True)

        @block.scalar
        def _(act):
            def evac_t(slot, q, gi, n_dense):
                act.wait_ge(t_done, gi + (q + 1))
                src = TP[:, q % 2 * HW:(q % 2 + 1) * HW]
                a, second = divmod(q - 1, 2)
                half = slice(second * HW, (second + 1) * HW)
                if q == 0:
                    dst = x2[:, :]
                elif q < 1 + 2 * NS:
                    dst = xs[:, a, half]
                elif q < GRP - 1:
                    dst = xa[:, slot % 2, a - NS, half]
                else:
                    dst = xq[:, slot % 4, :]
                    if n_dense is not None:
                        nc.scalar.activation(zsx[0:ND, bass.ds(n_dense * P, P)],
                                             src[0:ND, QW:QW + P], ACT.Copy).then_inc(dense_ready, 1)
                    src = src[:, 0:QW]
                nc.scalar.activation(dst, src, ACT.Copy).then_inc(t_evac, 1)

            def evac_z0(slot, g, tiles, sums):
                act.wait_ge(used[KIND[-1]], tiles + RING[KIND[-1]])
                for part in range(2):
                    nc.scalar.activation(hb[part * H:(part + 1) * H, slot, 0, :], Z0[0:H, :], ACT.Relu,
                                         bias=b0c[0:H, :]).then_inc(h_ready, 1)
                if sums is not None:
                    act.wait_ge(summed, sums)
                nc.scalar.activation(direct[H:O, :], Z0[H:O, :], ACT.Relu,
                                     bias=b0c[H:O, :]).then_inc(d0_ready, 1)

            def high_part(n_before, fix):
                act.wait_ge(raw_done, n_before + (fix + 1))
                act.wait_ge(used[CUT], n_before + (fix + 1))
                nc.scalar.activation(high[:, fix % RING[CUT], :], raw[:, fix % NRAW, :], ACT.Copy)\
                    .then_inc(high_done, 1)

            def high_parts(n, last, tiles):
                for s, p in tiles:
                    if KIND[p] == CUT:
                        high_part(n * (SPB * KIND.count(CUT)), fixed(CUT, s, last, p))

            act.sem_inc(z1h_ready, 1)
            act.wait_ge(small_in, NSMALL)
            act.wait_ge(const_ready, 7)
            l0 = [KIND[N1:].count(k) for k in (PLAIN, CUT)]
            for g in range(2):
                for q in range(GRP):
                    if g and q == 1:
                        act.wait_ge(plain_done, l0[PLAIN])
                    evac_t(g, q, g * GRP, 0 if g == 0 else None)
                for c in range(l0[CUT]):
                    high_part(0, g * l0[CUT] + c)
                evac_z0(g, g, (g + 1) * l0[KIND[-1]], 1 if g else None)
            high_parts(0, False, [(0, p) for p in range(HI_IN)])

            def one_block(n, last):
                for s in range(SPB):
                    g = n * SPB + s
                    tiles = list(window(s, last, HI_IN))
                    lead = HI_IN - PE_IN
                    for p in range(PE_IN, N1):
                        if tiles and (more(s, last) or p + lead < N1):
                            high_parts(n, last, [tiles.pop(0)])
                        for q in AFTER.get(p, []) if more(s, last) else []:
                            i, second = divmod(q - 1 - 2 * NS, 2)
                            if 0 <= i < NA and second == 0:
                                for kind, done in ((PLAIN, plain_done), (CUT, raw_done)):
                                    act.wait_ge(done, count(kind, n, s, last, NBJ * (i + 1)))
                            evac_t((s + 2) % 4, q, n * (SPB * GRP) + (s + 2) * GRP,
                                   n + 1 if s + 2 == SPB else None)
                    act.wait_ge(used[KIND[N1 - 1]],
                                count(KIND[N1 - 1], n, s, last, N1) + RING[KIND[N1 - 1]])
                    act.wait_ge(summed, n * SPB + (s + 2))
                    nc.scalar.activation(direct[0:H, :], Z1[0:H, :], ACT.Relu,
                                         bias=b1c[0:H, :]).then_inc(d1_ready, 1)
                    nc.scalar.activation(z1h[H:O, :], Z1[H:O, :], ACT.Relu,
                                         bias=b1c[H:O, :]).then_inc(z1h_ready, 1)
                    high_parts(n, last, tiles[:-lead] if more(s, last) else [])
                    if more(s, last):
                        evac_z0(s % 2, n * SPB + (s + 2), count(KIND[-1], n, s, last, STEP),
                                n * SPB + (s + 2))
                        tiles = tiles[-lead:]
                    high_parts(n, last, tiles)
                    act.wait_ge(s_done, g + 1)
                    act.wait_ge(r_free, g + 1)
                    nc.scalar.activation(r2[32:36, :], S[0:4, 0:QW], ACT.Relu,
                                         bias=b2c[:, :]).then_inc(r_ready, 1)

            with act.Fori(0, NBLK - 1) as n:
                one_block(n, False)
            one_block(NBLK - 1, True)

            with act.Fori(0, BATCH // HW) as c:
                for m in range(M1):
                    act.wait_ge(top1_done, c * M1 + (m + 1))
                    src = (Z0, Z1)[m // 2][:, m % 2 * HW:(m % 2 + 1) * HW]
                    nc.scalar.activation(h1[:, m, :], src, ACT.Relu, bias=bt1[:, m:m + 1])\
                        .then_inc(h1_ready, 1)
                for m in range(M2):
                    act.wait_ge(top2_done, c * M2 + (m + 1))
                    nc.scalar.activation(h2[:, m, :], TP[:, m * HW:(m + 1) * HW], ACT.Relu,
                                         bias=bt2[:, m:m + 1]).then_inc(h2_ready, 1)
                act.wait_ge(top3_done, c + 1)
                nc.scalar.activation(y[:, bass.ds(c * HW, HW)], G[0:1, :], ACT.Copy).then_inc(y_ready, 1)

        @block.vector
        def _(dve):
            dve.wait_ge(w_in, 3 * 16)
            w0v = w0s.rearrange("o (a b) -> o a b", b=F)
            for t, (ua, va) in enumerate(L0):
                dst = w0p[:, t * P:(t + 1) * P].rearrange("o (u h v) -> o u h v", h=2, v=8)
                for h in range(2):
                    a, b = 8 * ARR[ua][1 + h], 8 * ARR[va][1 + h]
                    one = w0v[:, a:a + 8, b:b + 8]
                    other = w0v[:, b:b + 8, a:a + 8].rearrange("o v u -> o u v")
                    if a == b:
                        nc.vector.tensor_copy(dst[:, :, h, :], one).then_inc(w_arranged, 1)
                    else:
                        nc.vector.tensor_tensor(dst[:, :, h, :], one, other, ALU.add)\
                            .then_inc(w_arranged, 1)
            w1v = w1s.rearrange("o (h v i r k) -> o h i r k v", v=16, i=NA, r=2, k=4)
            w1pv = w1p.rearrange("o (i j r k v) -> o j i r k v", i=NA, j=NBJ, r=2, k=4)
            for j in range(NBJ):
                for k in range(4):
                    nc.vector.tensor_copy(w1pv[:, j, :, :, k, :], w1v[:, (k + j) % 4, :, :, k, :])\
                        .then_inc(w_arranged, 1)
            nc.vector.memset(sel_q[:, :, :].rearrange("p a b -> p (a b)").bitcast(f32), 0.0)\
                .then_inc(sel_ready, 1)
            dve.wait_ge(const_ready, 7)
            dve.wait_ge(sel_ready, 1)
            for r in range(4):
                rows, half = slice(32 * r, 32 * r + 32), r // 2
                square = ident[rows, rows]
                for a, (kind, *blocks) in enumerate(ARR):
                    dst = sel[rows, a, :].rearrange("p (u h v) -> p u h v", h=2, v=8)
                    for h in range(2):
                        ones = ident[rows, 32 * r + 8 * blocks[h]:32 * r + 8 * blocks[h] + 8]
                        ones = ones.unsqueeze(2 if kind == "u" else 1).to_broadcast([32, 8, 8])
                        nc.vector.tensor_copy(dst[:, :, h, :], ones).then_inc(sel_ready, 1)
                for k in range(2):
                    q = 2 * half + k
                    nc.vector.tensor_copy(sel_q[rows, k, 32 * q:32 * q + 32], square)\
                        .then_inc(sel_ready, 1)
            dve.wait_ge(w_turned, 2)
            whole, parts = [], []
            for z in (Z1, TP):
                pairs = z[:, :].rearrange("p (t two o) -> p two t o", two=2, o=O)
                whole.append(pairs[:, PLAIN, :, :])
                parts.append(pairs[:, CUT, :, :])
            for t in range(N0):
                (whole, parts)[KIND[N1 + t]].append(
                    Z0[:, t * O:(t + 1) * O].rearrange("p (t o) -> p t o", t=1))
            at = 0
            for src in whole:
                nc.vector.tensor_copy(w_plain[:, at:at + src.shape[1], :], src).then_inc(w_ready, 1)
                at += src.shape[1]
            at = 0
            for src in parts:
                here = slice(at, at + src.shape[1])
                nc.vector.tensor_copy(w_high[:, here, :], src).then_inc(w_cut, 1)
                at += src.shape[1]
            dve.wait_ge(w_cut, len(parts))
            at = 0
            for src in parts:
                here = slice(at, at + src.shape[1])
                nc.vector.tensor_tensor(w_low[:, here, :], src, w_high[:, here, :].bitcast(f32),
                                        ALU.subtract).then_inc(w_ready, 1)
                at += src.shape[1]

            waiting = []

            def low_part():
                for n_before, fix in waiting:
                    dve.wait_ge(high_done, n_before + (fix + 1))
                    nc.vector.tensor_tensor(low[:, fix % RING[CUT], :], raw[:, fix % NRAW, :],
                                            high[:, fix % RING[CUT], :].bitcast(f32), ALU.subtract)\
                        .then_inc(low_done, 1)
                waiting.clear()

            def product(kind, n_before, fix, in0, in1):
                if kind == PLAIN:
                    dve.wait_ge(used[PLAIN], n_before + (fix + 1))
                    nc.vector.tensor_tensor(plain[:, fix % RING[PLAIN], :], in0, in1, ALU.mult)\
                        .then_inc(plain_done, 1)
                    low_part()
                else:
                    nc.vector.tensor_tensor(raw[:, fix % NRAW, :], in0, in1, ALU.mult)\
                        .then_inc(raw_done, 1)
                    low_part()
                    waiting.append((n_before, fix))

            def layer0(slot, t, n_before, fix, groups):
                def rows(a):
                    return xs[:, a, :] if a < NS else xa[:, slot, a - NS, :]

                dve.wait_ge(t_evac, groups + 1 + 2 * (max(L0[t]) + 1))
                product(KIND[N1 + t], n_before, fix, rows(L0[t][0]), rows(L0[t][1]))

            def sum_direct(rows, slot):
                nc.vector.tensor_reduce(dsum[rows, slot, :],
                                        direct[rows, :].rearrange("p (d b) -> p b d", b=P),
                                        AX.X, ALU.add).then_inc(summed, 1)

            def tiles_of(n, last, tiles):
                for s, p in tiles:
                    n_before, fix = n * (SPB * KIND.count(KIND[p])), fixed(KIND[p], s, last, p)
                    if p >= N1:
                        layer0(s % 2, p - N1, n_before, fix, n * (SPB * GRP) + (s + 2) * GRP)
                        continue
                    if p == 0:
                        dve.wait_ge(b_rot[s % 2], n * (16 * ROT * SPB // 2) + 16 * ROT * (s // 2 + 1))
                    i, j = L1[p]
                    product(KIND[p], n_before, fix, xa[:, s % 2, i, :], hb[:, s % 2, j, :])

            for g in range(2):
                for t in range(N0):
                    kind = KIND[N1 + t]
                    layer0(g, t, 0, g * KIND[N1:].count(kind) + KIND[N1:N1 + t].count(kind), g * GRP)
                dve.wait_ge(d0_ready, g + 1)
                sum_direct(slice(H, O), g)
            tiles_of(0, False, [(0, p) for p in range(DVE_IN)])
            low_part()

            def one_block(n, last):
                for s in range(SPB):
                    tiles_of(n, last, window(s, last, DVE_IN))
                    low_part()
                    dve.wait_ge(g_done, n * SPB + (s + 1))
                    nc.vector.tensor_tensor(v2[:, :], G[:, 0:QW], xq[:, s, :], ALU.mult)\
                        .then_inc(v_done, 1)
                    dve.wait_ge(d1_ready, n * SPB + (s + 1))
                    if more(s, last):
                        dve.wait_ge(d0_ready, n * SPB + (s + 3))
                        dve.wait_ge(zs_high, n * SPB + (s + 1))
                        sum_direct(slice(0, O), s % 2)
                    else:
                        dve.wait_ge(zs_low, n * SPB + (s - 1))
                        sum_direct(slice(0, H), s % 2)

            with dve.Fori(0, NBLK - 1) as n:
                one_block(n, False)
            one_block(NBLK - 1, True)

        @block.tensor
        def _(pe):
            for kind in (PLAIN, CUT):
                pe.sem_inc(used[kind], RING[kind])
            pe.wait_ge(const_ready, 7)
            pe.wait_ge(w_arranged, 2 * N0 + 4 * NBJ)
            for t in range(N0):
                last = nc.tensor.transpose(Z0[:, t * O:(t + 1) * O], w0p[:, t * P:(t + 1) * P],
                                           ident[:, :])
            last.then_inc(w_turned, 1)
            for t in range(N1):
                bank = (Z1, TP)[t // 8]
                last = nc.tensor.transpose(bank[:, t % 8 * O:(t % 8 + 1) * O], w1p[:, t * P:(t + 1) * P],
                                           ident[:, :])
            last.then_inc(w_turned, 1)

            def turn(s, q):
                bank = TP[:, q % 2 * HW:(q % 2 + 1) * HW]
                if q == 0:
                    for e in range(4):
                        cols = slice((s * 4 + e) * P, (s * 4 + e + 1) * P)
                        last = nc.tensor.transpose(bank[:, e * P:(e + 1) * P],
                                                   e_work[:, cols].bitcast(f32), ident[:, :])
                elif q < GRP - 1:
                    k, half = divmod(q - 1, 2)
                    rows = slice(64 * half, 64 * half + 64)
                    last = nc.tensor.matmul(bank, sel[rows, k, :], x2[rows, :], start=True, stop=True)
                else:
                    if s == 0:
                        nc.tensor.transpose(bank[0:ND, QW:QW + P], dense_work[:, :], ident[:, :])
                    for k in range(2):
                        last = nc.tensor.matmul(bank[:, 0:QW], sel_q[:, k, :], x2[:, k * QW:(k + 1) * QW],
                                                start=(k == 0), stop=(k == 1))
                last.then_inc(t_done, 1)

            def tile(n_before, fix, p):
                Z, first, end = (Z1, 0, N1) if p < N1 else (Z0, N1, STEP)
                kind = KIND[p]
                w = KIND[:p].count(kind)
                slot = fix % RING[kind]
                if kind == PLAIN:
                    passes = [(w_plain, plain, plain_done)]
                else:
                    passes = [(w_high, high, high_done), (w_low, high, None), (w_high, low, low_done)]
                for k, (wt, features, done) in enumerate(passes):
                    if done is not None:
                        pe.wait_ge(done, n_before + (fix + 1))
                    for b in range(2):
                        cols = slice(b * HW, (b + 1) * HW)
                        last = nc.tensor.matmul(Z[:, cols], wt[:, w, :], features[:, slot, cols],
                                                start=(p == first and k == 0),
                                                stop=(p == end - 1 and k == len(passes) - 1))
                last.then_inc(used[kind], 1)

            pe.wait_ge(w_ready, 2 + 2 + N0)
            pe.wait_ge(sel_ready, 1 + 4 * (2 * len(ARR) + 2))
            pe.wait_ge(e_ready, READY)
            for g in range(2):
                for q in range(GRP):
                    if g * GRP + q:
                        pe.wait_ge(t_evac, g * GRP + max(q - 1, 1 if q else 0))
                    turn(g, q)
                if g:
                    pe.wait_ge(d0_ready, g)
                for t in range(N0):
                    kind = KIND[N1 + t]
                    tile(0, g * KIND[N1:].count(kind) + KIND[N1:N1 + t].count(kind), N1 + t)

            def layer2_products(n, s):
                pe.wait_ge(z1h_ready, n * SPB + (s + 2))
                pe.sem_inc(pe_held, 1)
                for q in range(4):
                    last = nc.tensor.matmul(G[32 * q:32 * q + 32, 0:QW], w2t[H:O, :],
                                            z1h[H:O, q * QW:(q + 1) * QW], start=True, stop=True)
                last.then_inc(g_done, 1)

            def tile_of(n, s, last, p):
                if p == 0:
                    pe.wait_ge(z1h_ready, n * SPB + (s + 1))
                if p == N1:
                    pe.wait_ge(d0_ready, n * SPB + (s + 2))
                tile(n * (SPB * KIND.count(KIND[p])), fixed(KIND[p], s, last, p), p)

            for p in range(PE_IN):
                tile_of(0, 0, False, p)

            def one_block(n, last):
                for s in range(SPB):
                    after = (s, N1 + 1) if more(s, last) else (s + 1, 1)
                    for here, p in window(s, last, PE_IN):
                        tile_of(n, here, last, p)
                        for q in AFTER.get(p, []) if here == s and more(s, last) else []:
                            if q == 0 and s + 2 == SPB:
                                pe.wait_ge(e_ready, n * READY + 2 * READY)
                            pe.wait_ge(t_evac, n * (SPB * GRP) + (s + 2) * GRP + (1 if q == 1 else q - 1))
                            turn((s + 2) % SPB, q)
                        if (here, p) == after:
                            layer2_products(n, s)
                    if last and s == SPB - 1:
                        layer2_products(n, s)
                    pe.wait_ge(v_done, n * SPB + (s + 1))
                    nc.tensor.matmul(S[0:4, 0:QW], sel4[:, :], v2[:, :], start=True, stop=True)\
                        .then_inc(s_done, 1)

            with pe.Fori(0, NBLK - 1) as n:
                one_block(n, False)
            one_block(NBLK - 1, True)

            pe.wait_ge(zs_ready, NBLK)
            pe.wait_ge(zs_low, NSUP)
            pe.wait_ge(zs_high, NSUP)
            pe.wait_ge(dense_ready, NBLK)
            pe.wait_ge(z1h_ready, NSUP + 1)
            with pe.Fori(0, BATCH // HW) as c:
                for m in range(M1):
                    dst = (Z0, Z1)[m // 2][:, m % 2 * HW:(m % 2 + 1) * HW]
                    nc.tensor.matmul(dst, wt1a[:, m * P:(m + 1) * P], zs[:, bass.ds(c * HW, HW)],
                                     start=True, stop=False)
                    nc.tensor.matmul(dst, wt1b[:, m * P:(m + 1) * P], zsx[:, bass.ds(c * HW, HW)],
                                     start=False, stop=True).then_inc(top1_done, 1)
                for k in range(M1):
                    pe.wait_ge(h1_ready, c * M1 + (k + 1))
                    for m in range(M2):
                        last = nc.tensor.matmul(TP[:, m * HW:(m + 1) * HW], wt2[:, k, m * P:(m + 1) * P],
                                                h1[:, k, :], start=(k == 0), stop=(k == M1 - 1))
                        if k == M1 - 1:
                            last.then_inc(top2_done, 1)
                for k in range(M2):
                    pe.wait_ge(h2_ready, c * M2 + (k + 1))
                    last = nc.tensor.matmul(G[0:1, :], wt3[:, k:k + 1], h2[:, k, :],
                                            start=(k == 0), stop=(k == M2 - 1))
                last.then_inc(top3_done, 1)


_INS = (["dense_ctx", "ids"] + [f"tbl_{f}" for f in range(32)]
        + ["W_top1", "b_top1", "W_top2", "b_top2", "W_top3"]
        + [f"L0_rec_{w}" for w in ("W0", "b0", "W1", "b1", "W2", "b2")])


def kernel(**inputs):
    import numpy as _np
    import concourse.bacc as _bacc
    from concourse import mybir as _mybir
    from concourse.bass_utils import run_bass_kernel_spmd as _run

    nc = _bacc.Bacc("TRN2", target_bir_lowering=False, num_devices=1)
    arrays, aps = {}, {}
    for name in _INS:
        a = _np.ascontiguousarray(inputs[name])
        arrays[f"in_{name}"] = a
        aps[name] = nc.dram_tensor(f"in_{name}", a.shape, _mybir.dt.from_np(a.dtype), kind="ExternalInput").ap()
    batch = inputs["ids"].shape[0]
    out = nc.dram_tensor("out_y", (batch, 1), _mybir.dt.float32, kind="ExternalOutput").ap()
    build(nc, aps["dense_ctx"], aps["ids"], [aps[f"tbl_{f}"] for f in range(32)],
          *[aps[name] for name in _INS[34:]], out)
    r = _run(nc, [arrays], core_ids=[0])
    return r.results[0]["out_y"]
```

```python
import concourse.bass as bass
from concourse import mybir
from contextlib import ExitStack



def build(nc, dense_ctx, ids, tables, W_top1, b_top1, W_top2, b_top2, W_top3,
          W0, b0, W1, b1, W2, b2, out):
    f32 = mybir.dt.float32
    f32r = mybir.dt.float32r
    i32 = mybir.dt.int32
    ALU = mybir.AluOpType
    ACT = mybir.ActivationFunctionType
    AX = mybir.AxisListType

    BATCH, F = ids.shape
    D = tables[0].shape[1]
    ND = dense_ctx.shape[1]
    O = W0.shape[0]
    H = O // 2
    P = 128
    NBLK = BATCH // P
    DS = 8
    SPB = D // DS
    NSUP = NBLK * SPB
    W = DS * P
    HW = W // 2
    QW = W // 4
    OFF = (0, 0, F // 2, F // 2)
    FAR = (3, 7, 11, 15)
    NX, NH = 4, 4
    TURN = 4
    T1, T2 = W_top1.shape[1], W_top2.shape[1]
    M1, M2 = T1 // P, T2 // P

    L1 = [(i, t) for i in range(NX) for t in range(NH)]
    L0 = [0, None, 1, 2, 3]
    N0, N1 = len(L0), len(L1)
    STEP = N1 + N0
    PLAIN, CUT = 0, 1
    CUTS = (1, 3, 6, 9, 11, 13, 15)
    FOLD = N1 + L0.index(None)
    KIND = [CUT if p in CUTS or p == FOLD else PLAIN for p in range(STEP)]
    RING = [4, 4]
    NRAW = 2
    assert all(SPB * KIND.count(k) % RING[k] == 0 for k in (PLAIN, CUT))
    assert SPB * KIND.count(CUT) % NRAW == 0
    GRP = 2
    LOW_AFTER = 2
    PE_IN, DVE_IN, HI_IN = 4, 6, 6
    AFTER = {PE_IN: [0], PE_IN + 1: [1]}

    def runs(n, f):
        start = 0
        for p in range(1, n + 1):
            if p == n or any(b != a + 1 for a, b in zip(f(p - 1), f(p))):
                yield start, p - start
                start = p

    def x_row(i, p):
        b, r = divmod(p, 32)
        return (r + OFF[b] + (FAR[b] if i is None else i)) % F

    def PIECES(t):
        k = TURN * t
        return [(0, k, P - 16), (P - 16, P - 16 + k, 16 - k), (P - k, 0, k)]

    NPIECES = 3 * (NH - 1)
    NARR = 1 + 6 + sum(1 for i in L0 if i is not None for b in range(4) for _ in
                       runs(32, lambda r: (x_row(i, 32 * b + r), x_row(None, 32 * b + r)))) \
        + sum(1 for i, t in L1 for _ in runs(P, lambda p: (x_row(i, p), (p + TURN * t) % H)))
    ctx = ExitStack()
    with ctx:
        def sb(name, shape, dt=f32):
            return ctx.enter_context(nc.sbuf_tensor(name, shape, dt))

        def ps(name, shape):
            return ctx.enter_context(nc.psum_tensor(name, shape, f32))

        def sem(name):
            return ctx.enter_context(nc.semaphore(name))

        ids_all = sb("ids_all", [P, NBLK * F], i32)
        ids_cur = sb("ids_cur", [P, F], i32)
        dense_all = sb("dense_all", [P, NBLK * ND])
        e_gather = sb("e_gather", [P, F * D])
        e_work = sb("e_work", [P, D, P])
        dense_work = sb("dense_work", [P, 32])
        xs = sb("xs", [P, 2, NX, W])
        y_arr = sb("y_arr", [P, W])
        xh = sb("xh", [P, HW])
        xm = sb("xm", [P, HW])
        xq = sb("xq", [P, 4, QW])
        hs = sb("hs", [P, 2, NH, W])
        plain = sb("plain", [P, RING[PLAIN], W])
        raw = sb("raw", [P, NRAW, W])
        high = sb("high", [P, RING[CUT], W], f32r)
        low = sb("low", [P, RING[CUT], W], f32r)
        direct = sb("direct", [P, W])
        dsum = sb("dsum", [P, 2, P])
        z1h = sb("z1h", [P, HW])
        v2 = sb("v2", [P, QW])
        r2 = sb("r2", [P, QW])
        acc2 = sb("acc2", [P, QW])
        zs = sb("zs", [P, BATCH])
        zsx = sb("zsx", [64, BATCH])
        NPL, NCU = KIND.count(PLAIN), KIND.count(CUT) - 1
        w_plain = sb("w_plain", [P, NPL, O])
        w_high = sb("w_high", [P, NCU, O], f32r)
        w_low = sb("w_low", [P, NCU, O], f32r)
        w_fold = sb("w_fold", [P, 2, O], f32r)
        w2q = sb("w2q", [P, 2, P])
        wt1a = sb("wt1a", [P, T1])
        wt1b = sb("wt1b", [64, T1])
        wt2 = sb("wt2", [P, M1, T2])
        wt3 = sb("wt3", [P, M2])
        b0c = sb("b0c", [P, 1])
        b1c = sb("b1c", [P, 1])
        b2c = sb("b2c", [4, 1])
        bt1 = sb("bt1", [P, M1])
        bt2 = sb("bt2", [P, M2])
        ident = sb("ident", [P, P])
        low_rows = sb("low_rows", [P, 1])
        sel4 = sb("sel4", [P, 4])
        stage = hs[:, :, :, :].rearrange("p a b c -> p (a b c)")
        w0s = stage[:, 0:F * F]
        w1s = stage[:, F * F:F * F + H * F]
        w1p = stage[:, F * F + H * F:F * F + 2 * H * F]
        w0p = stage[:, F * F + 2 * H * F:F * F + 2 * H * F + (N0 + 1) * P]
        fold_at = F * F + 2 * H * F + (N0 + 1) * P
        wf, wf_high, wf_low = (stage[:, fold_at + k * 16:fold_at + k * 16 + 16] for k in range(3))
        h1 = stage[:, 0:M1 * HW].rearrange("p (m c) -> p m c", m=M1)
        h2 = stage[:, M1 * HW:(M1 + M2) * HW].rearrange("p (m c) -> p m c", m=M2)
        y_xm = [(y_arr[:, :], xm[:, :]), (hs[:, 1, NH - 2, :], hs[:, 1, NH - 1, 0:HW])]
        x_halves = [xh[:, :], hs[:, 1, NH - 1, HW:W]]
        y = stage[0:1, (M1 + M2) * HW:(M1 + M2) * HW + BATCH]

        Z0 = ps("Z0", [P, W])
        Z1 = ps("Z1", [P, W])
        TP = ps("TP", [P, 2 * HW])
        G = ps("G", [P, HW])
        S = ps("S", [P, HW])

        ids_in = sem("ids_in")
        dense_in = sem("dense_in")
        w_in = sem("w_in")
        small_in = sem("small_in")
        const_ready = sem("const_ready")
        ident_ready = sem("ident_ready")
        cleared = sem("cleared")
        masked = sem("masked")
        wf_step = sem("wf_step")
        pool_step = sem("pool_step")
        gathered = sem("gathered")
        pool_held = sem("pool_held")
        sp_held = sem("sp_held")
        e_ready = sem("e_ready")
        w_arranged = sem("w_arranged")
        w_turned = sem("w_turned")
        w_cut = sem("w_cut")
        w_ready = sem("w_ready")
        t_done = sem("t_done")
        t_evac = sem("t_evac")
        dense_ready = sem("dense_ready")
        plain_done = sem("plain_done")
        raw_done = sem("raw_done")
        high_done = sem("high_done")
        low_done = sem("low_done")
        used = [sem("plain_used"), sem("cut_used")]
        h_ready = sem("h_ready")
        d0_ready = sem("d0_ready")
        y_in = [sem("y_in0"), sem("y_in1")]
        x_in = [[None] + [sem(f"x_in{slot}_{i}") for i in range(1, NX)] for slot in range(2)]
        h_in = [sem("h_in0"), sem("h_in1")]
        z1h_ready = sem("z1h_ready")
        d1_ready = sem("d1_ready")
        summed = sem("summed")
        zs_low = sem("zs_low")
        zs_high = sem("zs_high")
        g_done = sem("g_done")
        v_done = sem("v_done")
        s_done = sem("s_done")
        r_ready = sem("r_ready")
        r_free = sem("r_free")
        zs_ready = sem("zs_ready")
        top1_done = sem("top1_done")
        h1_ready = sem("h1_ready")
        top2_done = sem("top2_done")
        h2_ready = sem("h2_ready")
        top3_done = sem("top3_done")
        y_ready = sem("y_ready")
        y_out = sem("y_out")

        def count(kind, n, s, last, p):
            return n * (SPB * KIND.count(kind)) + fixed(kind, s, last, p)

        def fixed(kind, s, last, p):
            l0 = KIND[N1:].count(kind)
            return 2 * l0 + s * KIND.count(kind) + KIND[:p].count(kind) \
                - (l0 if last and s == SPB - 1 else 0)

        def window(s, last, into):
            yield from ((s, p) for p in range(into, STEP if more(s, last) else N1))
            if not (last and s == SPB - 1):
                yield from ((s + 1, p) for p in range(into))

        def more(s, last):
            return not (last and s + 2 >= SPB)

        def arrangement(sup):
            src = e_gather[:, :].rearrange("p (f d) -> p d f", d=D)[:, sup * DS:(sup + 1) * DS, :]
            dst = e_work[:, sup * DS:(sup + 1) * DS, :].rearrange("p d (h b r) -> p d h b r", h=2, b=2)
            for half, first, to, n in ((0, 0, 0, F), (1, F // 2, 0, F // 2), (1, 0, F // 2, F // 2)):
                yield (dst[:, :, half, :, to:to + n],
                       src[:, :, first:first + n].unsqueeze(2).to_broadcast([P, DS, 2, n]))

        def columns(p):
            return slice(0, HW) if p == FOLD else slice(0, W)

        block = ctx.enter_context(nc.Block())

        @block.sync
        def _(sp):
            sp.dma_start(ids_all[:, :].rearrange("p (n f) -> p n f", f=F),
                         ids.rearrange("(n p) f -> p n f", p=P)).then_inc(ids_in, 16)
            sp.dma_start(dense_all[:, :].rearrange("p (n f) -> p n f", f=ND),
                         dense_ctx.rearrange("(n p) f -> p n f", p=P)).then_inc(dense_in, 16)
            sp.dma_start(w0s, W0).then_inc(w_in, 16)
            sp.dma_start(w1s[0:H, :], W1[H:O, :]).then_inc(w_in, 16)
            sp.dma_start(w1s[H:O, :], W1[0:H, :]).then_inc(w_in, 16)
            loads = [
                (b0c[:, :], b0.rearrange("(p a) -> p a", a=1)),
                (b1c[0:H, :], b1[H:O].rearrange("(p a) -> p a", a=1)),
                (b1c[H:O, :], b1[0:H].rearrange("(p a) -> p a", a=1)),
                (b2c[:, :], b2.rearrange("(p a) -> p a", a=1).to_broadcast([4, 1])),
                (wt1a[0:H, :], W_top1[H:2 * H, :]),
                (wt1a[H:O, :], W_top1[0:H, :]),
                (wt2[:, :, :], W_top2.rearrange("(k p) n -> p k n", p=P)),
                (wt3[:, :], W_top3.rearrange("(k p) a -> p (k a)", p=P)),
                (bt1[:, :], b_top1.rearrange("(k p) -> p k", p=P)),
                (bt2[:, :], b_top2.rearrange("(k p) -> p k", p=P)),
            ]
            for dst, src in loads:
                sp.dma_start(dst, src, allow_slow_non_contiguous=dst.shape[-1] < 8)\
                    .then_inc(small_in, 16)
            sp.wait_ge(const_ready, 3)
            w2v = W2.rearrange("a (h m) -> (a h) m", m=F)
            for q in range(4):
                half, c = divmod(q, 2)
                for at, n in runs(F, lambda r: (x_row(0, 32 * q + r),)):
                    m = x_row(0, 32 * q + at)
                    sp.dma_start(w2q[half * H:(half + 1) * H, c, 32 * q + at:32 * q + at + n],
                                 w2v[:, m:m + n]).then_inc(small_in, 16)
            sp.dma_start(wt1b[0:ND, :], W_top1[2 * H + 1:2 * H + 1 + ND, :]).then_inc(small_in, 16)
            sp.dma_start(wt1b[32:36, :], W_top1[2 * H:2 * H + 1, :].to_broadcast([4, T1])).then_inc(small_in, 16)

            def wait(semaphore, value):
                sp.wait_ge(semaphore, value)
                sp.sem_inc(sp_held, 1)

            def spread_y(slot, m, used, y_dst, xm_dst):
                x0 = xs[:, slot, 0, :]
                wait(t_evac, m * GRP + GRP)
                used()
                for b in range(4):
                    src = 64 * (b // 2) + FAR[b]
                    sp.dma_start(y_dst[32 * b:32 * b + 32, :], x0[src:src + 32, :]).then_inc(y_in[slot], 16)
                for half in range(2):
                    sp.dma_start(xm_dst[64 * half:64 * half + 64, :],
                                 x0[64 - 64 * half:128 - 64 * half, half * HW:(half + 1) * HW])\
                        .then_inc(y_in[slot], 16)

            def spread_x(slot, m, used):
                wait(t_evac, m * GRP + GRP)
                for i in range(1, NX):
                    used(i)
                    for b in range(4):
                        src = 64 * (b // 2) + i
                        sp.dma_start(xs[32 * b:32 * b + 32, slot, i, :],
                                     xs[src:src + 32, slot, 0, :]).then_inc(x_in[slot][i], 16)

            def spread_h(slot, m):
                wait(h_ready, m * 2 + 2)
                for t in range(1, NH):
                    for dst, src, n in PIECES(t):
                        sp.dma_start(hs[dst:dst + n, slot, t, :], hs[src:src + n, slot, 0, :])\
                            .then_inc(h_in[slot], 16)

            spread_y(0, 0, lambda: None, *y_xm[0])
            spread_x(0, 0, lambda i: None)
            spread_y(1, 1, lambda: None, *y_xm[1])
            spread_x(1, 1, lambda i: None)
            for m in range(2):
                spread_h(m, m)

            def one_block(n, last):
                for s in range(SPB):
                    if not more(s, last):
                        continue

                    def products(p):
                        wait(plain_done, count(PLAIN, n, s, last, p))
                        wait(raw_done, count(CUT, n, s, last, p))
                    spread_y(s % 2, n * SPB + (s + 2), lambda: products(0), *y_xm[0])
                    spread_x(s % 2, n * SPB + (s + 2), lambda i: products(NH * (i + 1)))
                    spread_h(s % 2, n * SPB + (s + 2))

            with sp.Fori(0, NBLK - 1) as n:
                one_block(n, False)
            one_block(NBLK - 1, True)
            sp.wait_ge(y_ready, BATCH // HW)
            sp.dma_start(out.rearrange("b a -> a b"), y).then_inc(y_out, 16)
            sp.wait_ge(y_out, 16)

        NSMALL = (12 + 6) * 16
        READY = 3 * SPB + 1

        @block.gpsimd
        def _(pool):
            pool.sem_inc(r_free, 1)

            def held():
                pool.sem_inc(pool_held, 1)

            def gather(m, fields):
                held()
                for f in fields:
                    nc.gpsimd.indirect_dma_start(
                        e_gather[:, f * D:(f + 1) * D], None, tables[f],
                        bass.IndirectOffsetOnAxis(ids_cur[:, f:f + 1], 0)).then_inc(gathered, 16)
                pool.wait_ge(gathered, m * (16 * F) + 16 * (fields[-1] + 1))

            nc.gpsimd.memset(wt1b[:, :], 0.0).then_inc(const_ready, 1)
            nc.gpsimd.memset(w2q[:, :, :], 0.0).then_inc(const_ready, 1)
            nc.gpsimd.memset(dense_work[:, :], 0.0).then_inc(const_ready, 1)
            nc.gpsimd.memset(ident[:, :], 0.0).then_inc(pool_step, 1)
            pool.wait_ge(pool_step, 1)
            nc.gpsimd.affine_select(out=ident[:, :], in_=ident[:, :], compare_op=ALU.not_equal,
                                    fill=1.0, base=0, pattern=[[-1, P]], channel_multiplier=1)\
                .then_inc(ident_ready, 1)
            pool.wait_ge(ids_in, 16)
            nc.gpsimd.tensor_copy(ids_cur[:, :], ids_all[:, 0:F]).then_inc(pool_step, 1)
            pool.wait_ge(pool_step, 2)
            gather(0, range(F))

            def arrange(m):
                for sup in range(SPB):
                    for dst, src in arrangement(sup):
                        nc.gpsimd.tensor_copy(dst, src).then_inc(e_ready, 1)
                nc.gpsimd.tensor_copy(dense_work[:, 0:ND], dense_all[:, bass.ds(m * ND, ND)])\
                    .then_inc(e_ready, 1)
                pool.wait_ge(e_ready, m * READY + READY)

            def fetch_ids(m, at):
                nc.gpsimd.tensor_copy(ids_cur[:, :], ids_all[:, bass.ds(m * F, F)])\
                    .then_inc(pool_step, 1)
                at += 1
                pool.wait_ge(pool_step, at)
                return at

            at = fetch_ids(1, 2)
            pool.wait_ge(e_ready, READY)
            gather(1, range(F))

            BEGUN = at
            lo, hi = slice(0, H), slice(H, O)

            def add_direct(rows, count, slot, m, s):
                dst, src = zs[rows, bass.ds(m * P, P)], dsum[rows, slot, :]
                held()
                if s == 0:
                    nc.gpsimd.tensor_copy(dst, src).then_inc(count, 1)
                else:
                    nc.gpsimd.tensor_tensor(dst, dst, src, ALU.add).then_inc(count, 1)
                pool.wait_ge(count, m * SPB + (s + 1))

            def add_both(n, s, last):
                pool.wait_ge(summed, n * SPB + (s + 3))
                add_direct(lo, zs_low, s % 2, n, s)
                if more(s, last):
                    add_direct(hi, zs_high, s % 2, n + (s + 2) // SPB, (s + 2) % SPB)

            def add_layer2(n, s):
                rows = slice(32, 36)
                pool.wait_ge(r_ready, n * SPB + (s + 1))
                if s == 0:
                    held()
                    nc.gpsimd.tensor_copy(acc2[rows, :], r2[rows, :]).then_inc(r_free, 1)
                else:
                    nc.gpsimd.tensor_tensor(acc2[rows, :], acc2[rows, :], r2[rows, :], ALU.add)\
                        .then_inc(r_free, 1)
                pool.wait_ge(r_free, n * SPB + (1 + s + 1))
                if s == SPB - 1:
                    held()
                    nc.gpsimd.tensor_tensor(zsx[rows, bass.ds(n * P, P)], acc2[rows, 0:P],
                                            acc2[rows, P:2 * P], ALU.add).then_inc(zs_ready, 1)
                    pool.wait_ge(zs_ready, n + 1)

            BLOCK = 1
            SPREAD = {1: range(0, 8), 2: range(8, 20), 3: range(20, F)}

            def one_block(n, at, copy, fetch, last):
                for s in range(SPB):
                    if s == 1 and copy:
                        pool.wait_ge(t_done, n * (SPB * GRP) + SPB * GRP)
                        held()
                        arrange(n + 1)
                    if s == 1 and fetch:
                        at = fetch_ids(n + 2, at)
                    if fetch and s in SPREAD:
                        gather(n + 2, SPREAD[s])
                    add_both(n, s, last)
                    add_layer2(n, s)
                return at

            for g in range(2):
                pool.wait_ge(summed, g + 1)
                add_direct(hi, zs_high, g, 0, g)
            with pool.Fori(0, NBLK - 2) as n:
                one_block(n, n * BLOCK + BEGUN, True, True, False)
            at = one_block(NBLK - 2, (NBLK - 2) * BLOCK + BEGUN, True, False, False)
            one_block(NBLK - 1, at, False, False, True)

        @block.scalar
        def _(act):
            def evac_t(slot, q, gi, n_dense, xh_dst):
                act.wait_ge(t_done, gi + (q + 1))
                if q == 0 and n_dense is not None:
                    nc.scalar.activation(zsx[0:ND, bass.ds(n_dense * P, P)],
                                         S[32:32 + ND, QW:QW + P], ACT.Copy).then_inc(dense_ready, 1)
                for c in range(2):
                    rows = slice(32 * (2 * q + c), 32 * (2 * q + c) + 32)
                    nc.scalar.activation(xq[rows, slot, :],
                                         TP[rows, q * HW + c * QW:q * HW + (c + 1) * QW], ACT.Copy)
                half = slice(q * HW, (q + 1) * HW)
                rows = slice(64 * q, 64 * q + 64)
                nc.scalar.activation(xh_dst[rows, :], TP[rows, half], ACT.Copy)
                nc.scalar.activation(xs[:, slot % 2, 0, half], TP[:, half], ACT.Copy)\
                    .then_inc(t_evac, 1)

            def evac_z0(slot, g, tiles, sums):
                act.wait_ge(used[KIND[-1]], tiles + RING[KIND[-1]])
                for part in range(2):
                    nc.scalar.activation(hs[part * H:(part + 1) * H, slot, 0, :], Z0[0:H, :], ACT.Relu,
                                         bias=b0c[0:H, :]).then_inc(h_ready, 1)
                if sums is not None:
                    act.wait_ge(summed, sums)
                nc.scalar.activation(direct[H:O, :], Z0[H:O, :], ACT.Relu,
                                     bias=b0c[H:O, :]).then_inc(d0_ready, 1)

            def high_part(n_before, fix, cols):
                act.wait_ge(raw_done, n_before + (fix + 1))
                act.wait_ge(used[CUT], n_before + (fix + 1))
                nc.scalar.activation(high[:, fix % RING[CUT], cols], raw[:, fix % NRAW, cols], ACT.Copy)\
                    .then_inc(high_done, 1)

            def high_parts(n, last, tiles):
                for s, p in tiles:
                    if KIND[p] == CUT:
                        high_part(n * (SPB * KIND.count(CUT)), fixed(CUT, s, last, p), columns(p))

            act.sem_inc(z1h_ready, 1)
            act.wait_ge(dense_in, 16)
            act.wait_ge(const_ready, 3)
            nc.scalar.activation(dense_work[:, 0:ND], dense_all[:, 0:ND], ACT.Copy).then_inc(e_ready, 1)
            act.wait_ge(small_in, NSMALL)
            act.wait_ge(cleared, 6)
            l0 = [KIND[N1:].count(k) for k in (PLAIN, CUT)]
            for g in range(2):
                for q in range(GRP):
                    evac_t(g, q, g * GRP, 0 if g == 0 else None, x_halves[g])
            for g in range(2):
                for c, p in enumerate(p for p in range(N1, STEP) if KIND[p] == CUT):
                    high_part(0, g * l0[CUT] + c, columns(p))
                evac_z0(g, g, (g + 1) * l0[KIND[-1]], 1 if g else None)
            high_parts(0, False, [(0, p) for p in range(HI_IN)])

            def one_block(n, last):
                for s in range(SPB):
                    g = n * SPB + s
                    tiles = list(window(s, last, HI_IN))
                    lead = HI_IN - PE_IN
                    for p in range(PE_IN, N1):
                        if tiles and (more(s, last) or p + lead < N1):
                            high_parts(n, last, [tiles.pop(0)])
                        for q in AFTER.get(p, []) if more(s, last) else []:
                            if q == 0:
                                for kind, done in ((PLAIN, plain_done), (CUT, raw_done)):
                                    act.wait_ge(done, count(kind, n, s, last, NH))
                            evac_t((s + 2) % 4, q, n * (SPB * GRP) + (s + 2) * GRP,
                                   n + 1 if s + 2 == SPB else None, x_halves[0])
                    act.wait_ge(used[KIND[N1 - 1]],
                                count(KIND[N1 - 1], n, s, last, N1) + RING[KIND[N1 - 1]])
                    act.wait_ge(summed, n * SPB + (s + 2))
                    nc.scalar.activation(direct[0:H, :], Z1[0:H, :], ACT.Relu,
                                         bias=b1c[0:H, :]).then_inc(d1_ready, 1)
                    for half in range(2):
                        last_half = nc.scalar.activation(
                            z1h[half * H:(half + 1) * H, :], Z1[H:O, half * HW:(half + 1) * HW],
                            ACT.Relu, bias=b1c[H:O, :])
                    last_half.then_inc(z1h_ready, 1)
                    high_parts(n, last, tiles[:-lead] if more(s, last) else [])
                    if more(s, last):
                        evac_z0(s % 2, n * SPB + (s + 2), count(KIND[-1], n, s, last, STEP),
                                n * SPB + (s + 2))
                        tiles = tiles[-lead:]
                    high_parts(n, last, tiles)
                    act.wait_ge(s_done, g + 1)
                    act.wait_ge(r_free, g + 1)
                    nc.scalar.activation(r2[32:36, :], S[0:4, 0:QW], ACT.Relu,
                                         bias=b2c[:, :]).then_inc(r_ready, 1)

            with act.Fori(0, NBLK - 1) as n:
                one_block(n, False)
            one_block(NBLK - 1, True)

            with act.Fori(0, BATCH // HW) as c:
                for m in range(M1):
                    act.wait_ge(top1_done, c * M1 + (m + 1))
                    src = (Z0, Z1)[m // 2][:, m % 2 * HW:(m % 2 + 1) * HW]
                    nc.scalar.activation(h1[:, m, :], src, ACT.Relu, bias=bt1[:, m:m + 1])\
                        .then_inc(h1_ready, 1)
                for m in range(M2):
                    act.wait_ge(top2_done, c * M2 + (m + 1))
                    nc.scalar.activation(h2[:, m, :], TP[:, m * HW:(m + 1) * HW], ACT.Relu,
                                         bias=bt2[:, m:m + 1]).then_inc(h2_ready, 1)
                act.wait_ge(top3_done, c + 1)
                nc.scalar.activation(y[:, bass.ds(c * HW, HW)], G[0:1, :], ACT.Copy).then_inc(y_ready, 1)

        @block.vector
        def _(dve):
            nc.vector.memset(zsx[:, :], 0.0).then_inc(cleared, 1)
            nc.vector.memset(sel4[:, :], 0.0).then_inc(cleared, 1)
            dve.wait_ge(cleared, 2)
            for q in range(4):
                nc.vector.memset(sel4[32 * q:32 * q + 32, q:q + 1], 1.0).then_inc(cleared, 1)
            nc.vector.memset(low_rows[:, :], 0.0).then_inc(masked, 1)
            dve.wait_ge(masked, 1)
            for half in range(2):
                nc.vector.memset(low_rows[64 * half + 32:64 * half + 64, :], 1.0).then_inc(masked, 1)
            dve.wait_ge(masked, 3)
            dve.wait_ge(w_in, 3 * 16)
            nc.vector.memset(w0p, 0.0).then_inc(w_arranged, 1)
            dve.wait_ge(w_arranged, 1)

            def diagonal(w, a, b, n):
                at = a * F + b
                return w[:, at:at + (F + 1) * (n - 1) + 1:F + 1]

            for t, i in enumerate(L0):
                if i is None:
                    nc.vector.tensor_tensor(wf, diagonal(w0s, 0, F // 2, 16), diagonal(w0s, F // 2, 0, 16),
                                            ALU.add).then_inc(wf_step, 1)
                    dve.wait_ge(wf_step, 1)
                    nc.vector.tensor_copy(wf_high.bitcast(f32r), wf).then_inc(wf_step, 1)
                    dve.wait_ge(wf_step, 2)
                    nc.vector.tensor_tensor(wf_low, wf, wf_high, ALU.subtract).then_inc(wf_step, 1)
                    dve.wait_ge(wf_step, 3)
                    for half in range(2):
                        for k, (part, sign) in enumerate(((wf_high, -1.0), (wf_low, -1.0), (wf_high, 1.0))):
                            at = (t + half * (N0 - t)) * P + 64 * half + 16 * k
                            nc.vector.tensor_scalar(w0p[:, at:at + 16], part, sign, None, ALU.mult)\
                                .then_inc(w_arranged, 1)
                    continue
                pieces = [(p, n, x_row(i, p), x_row(None, p)) for b in range(4) for p, n in
                          ((32 * b + p, n) for p, n in
                           runs(32, lambda r: (x_row(i, 32 * b + r), x_row(None, 32 * b + r))))]
                for p, n, a, b in pieces:
                    dst = w0p[:, t * P + p:t * P + p + n]
                    if a == b:
                        nc.vector.tensor_copy(dst, diagonal(w0s, a, b, n)).then_inc(w_arranged, 1)
                    else:
                        nc.vector.tensor_tensor(dst, diagonal(w0s, a, b, n), diagonal(w0s, b, a, n),
                                                ALU.add).then_inc(w_arranged, 1)
            for tile, (i, t) in enumerate(L1):
                for p, n in runs(P, lambda p: (x_row(i, p), (p + TURN * t) % H)):
                    nc.vector.tensor_copy(w1p[:, tile * P + p:tile * P + p + n],
                                          diagonal(w1s, (p + TURN * t) % H, x_row(i, p), n))\
                        .then_inc(w_arranged, 1)
            dve.wait_ge(w_turned, 2)
            turned = [(Z1, TP)[p // 8][:, p % 8 * O:(p % 8 + 1) * O] for p in range(N1)] \
                + [Z0[:, t * O:(t + 1) * O] for t in range(N0)]
            at = [0, 0]
            parts = []
            for p, (kind, src) in enumerate(zip(KIND, turned)):
                if p == FOLD:
                    continue
                if kind == PLAIN:
                    nc.vector.tensor_copy(w_plain[:, at[PLAIN], :], src).then_inc(w_ready, 1)
                else:
                    nc.vector.tensor_copy(w_high[:, at[CUT], :], src).then_inc(w_cut, 1)
                    parts.append(src)
                at[kind] += 1
            dve.wait_ge(w_cut, NCU)
            for k, src in enumerate(parts):
                nc.vector.tensor_tensor(w_low[:, k, :], src, w_high[:, k, :].bitcast(f32),
                                        ALU.subtract).then_inc(w_ready, 1)
            for half, t in enumerate((FOLD - N1, N0)):
                nc.vector.tensor_copy(w_fold[:, half, :], Z0[:, t * O:(t + 1) * O]).then_inc(w_ready, 1)

            dve.wait_ge(gathered, 16 * F)
            dve.wait_ge(e_ready, 1)
            for sup in range(SPB):
                for dst, src in arrangement(sup):
                    nc.vector.tensor_copy(dst, src).then_inc(e_ready, 1)

            waiting = []

            def low_parts(after=0):
                while waiting and waiting[0][3] >= after:
                    n_before, fix, fold, _ = waiting.pop(0)
                    dve.wait_ge(high_done, n_before + (fix + 1))
                    raw_part, high_part = raw[:, fix % NRAW, :], high[:, fix % RING[CUT], :].bitcast(f32)
                    dst = low[:, fix % RING[CUT], :]
                    if fold:
                        nc.vector.scalar_tensor_tensor(
                            dst[:, 0:HW], raw_part[:, 0:HW], low_rows[:, 0:1], high_part[:, 0:HW],
                            ALU.mult, ALU.subtract).then_inc(low_done, 1)
                    else:
                        nc.vector.tensor_tensor(dst, raw_part, high_part, ALU.subtract)\
                            .then_inc(low_done, 1)

            def product(kind, n_before, fix, in0, in1, fold=False):
                if kind == PLAIN:
                    dve.wait_ge(used[PLAIN], n_before + (fix + 1))
                    nc.vector.tensor_tensor(plain[:, fix % RING[PLAIN], :], in0, in1, ALU.mult)\
                        .then_inc(plain_done, 1)
                else:
                    if fix >= NRAW:
                        dve.wait_ge(low_done, n_before + (fix - NRAW + 1))
                    cols = slice(0, HW) if fold else slice(0, W)
                    nc.vector.tensor_tensor(raw[:, fix % NRAW, cols], in0, in1, ALU.mult)\
                        .then_inc(raw_done, 1)
                waiting[:] = [(*w[:3], w[3] + 1) for w in waiting]
                low_parts(LOW_AFTER)
                if kind == CUT:
                    waiting.append((n_before, fix, fold, 0))

            def layer0(slot, t, n_before, fix, nth, y, xm, xh):
                i = L0[t]
                if t == 0:
                    dve.wait_ge(y_in[slot], nth * (16 * 6) + 16 * 6)
                elif i is not None:
                    dve.wait_ge(x_in[slot][i], nth * (16 * 4) + 16 * 4)
                if i is None:
                    product(KIND[N1 + t], n_before, fix, xh, xm, True)
                else:
                    product(KIND[N1 + t], n_before, fix, xs[:, slot, i, :], y)

            def sum_direct(rows, slot):
                nc.vector.tensor_reduce(dsum[rows, slot, :],
                                        direct[rows, :].rearrange("p (d b) -> p b d", b=P),
                                        AX.X, ALU.add).then_inc(summed, 1)

            def tiles_of(n, last, tiles):
                for s, p in tiles:
                    n_before, fix = n * (SPB * KIND.count(KIND[p])), fixed(KIND[p], s, last, p)
                    if p >= N1:
                        layer0(s % 2, p - N1, n_before, fix,
                               n * (SPB // 2) + (s + 2) // 2, *y_xm[0], x_halves[0])
                        continue
                    if p == 0:
                        per = 16 * NPIECES
                        dve.wait_ge(h_in[s % 2], n * (per * SPB // 2) + per * (s // 2 + 1))
                    i, t = L1[p]
                    product(KIND[p], n_before, fix, xs[:, s % 2, i, :], hs[:, s % 2, t, :])

            for g in range(2):
                for t in range(N0):
                    kind = KIND[N1 + t]
                    layer0(g, t, 0, g * KIND[N1:].count(kind) + KIND[N1:N1 + t].count(kind), 0, *y_xm[g],
                           x_halves[g])
            dve.wait_ge(d0_ready, 1)
            sum_direct(slice(H, O), 0)
            tiles_of(0, False, [(0, p) for p in range(DVE_IN)])
            low_parts()
            dve.wait_ge(d0_ready, 2)
            sum_direct(slice(H, O), 1)

            def one_block(n, last):
                for s in range(SPB):
                    tiles_of(n, last, window(s, last, DVE_IN))
                    low_parts()
                    dve.wait_ge(g_done, n * SPB + (s + 1))
                    nc.vector.tensor_tensor(v2[:, :], G[:, 0:QW], xq[:, s, :], ALU.mult)\
                        .then_inc(v_done, 1)
                    dve.wait_ge(d1_ready, n * SPB + (s + 1))
                    if more(s, last):
                        dve.wait_ge(d0_ready, n * SPB + (s + 3))
                        dve.wait_ge(zs_high, n * SPB + (s + 1))
                        sum_direct(slice(0, O), s % 2)
                    else:
                        dve.wait_ge(zs_low, n * SPB + (s - 1))
                        sum_direct(slice(0, H), s % 2)

            with dve.Fori(0, NBLK - 1) as n:
                one_block(n, False)
            one_block(NBLK - 1, True)

        @block.tensor
        def _(pe):
            for kind in (PLAIN, CUT):
                pe.sem_inc(used[kind], RING[kind])
            pe.wait_ge(ident_ready, 1)
            pe.wait_ge(w_arranged, NARR)
            for t in range(N0 + 1):
                last = nc.tensor.transpose(Z0[:, t * O:(t + 1) * O], w0p[:, t * P:(t + 1) * P],
                                           ident[:, :])
            last.then_inc(w_turned, 1)
            for t in range(N1):
                bank = (Z1, TP)[t // 8]
                last = nc.tensor.transpose(bank[:, t % 8 * O:(t % 8 + 1) * O], w1p[:, t * P:(t + 1) * P],
                                           ident[:, :])
            last.then_inc(w_turned, 1)

            def turn(s, q):
                if s == 0 and q == 0:
                    nc.tensor.matmul(S[32:64, QW:QW + P], dense_work[:, :], ident[:, :],
                                     start=True, stop=True)
                for e in range(4):
                    last = nc.tensor.transpose(TP[:, q * HW + e * P:q * HW + (e + 1) * P],
                                               e_work[:, DS * s + 4 * q + e, :], ident[:, :])
                last.then_inc(t_done, 1)

            def tile(n_before, fix, p):
                Z, first, end = (Z1, 0, N1) if p < N1 else (Z0, N1, STEP)
                kind = KIND[p]
                slot = fix % RING[kind]
                if p == FOLD:
                    passes = [(None, low, low_done)]
                elif kind == PLAIN:
                    passes = [(w_plain, plain, plain_done)]
                else:
                    passes = [(w_high, high, high_done), (w_low, high, None), (w_high, low, low_done)]
                w = sum(1 for q in range(p) if KIND[q] == kind and q != FOLD)
                for k, (wt, features, done) in enumerate(passes):
                    if done is not None:
                        pe.wait_ge(done, n_before + (fix + 1))
                    for b in range(2):
                        cols = slice(b * HW, (b + 1) * HW)
                        weights = w_fold[:, b, :] if p == FOLD else wt[:, w, :]
                        last = nc.tensor.matmul(Z[:, cols], weights,
                                                features[:, slot, slice(0, HW) if p == FOLD else cols],
                                                start=(p == first and k == 0),
                                                stop=(p == end - 1 and k == len(passes) - 1))
                last.then_inc(used[kind], 1)

            pe.wait_ge(w_ready, NPL + NCU + 2)
            for g in range(2):
                pe.wait_ge(e_ready, 1 + 3 * (g + 1))
                for q in range(GRP):
                    if g:
                        pe.wait_ge(t_evac, q + 1)
                    turn(g, q)
            pe.wait_ge(small_in, NSMALL)
            pe.wait_ge(cleared, 6)
            for g in range(2):
                if g:
                    pe.wait_ge(d0_ready, g)
                for t in range(N0):
                    kind = KIND[N1 + t]
                    tile(0, g * KIND[N1:].count(kind) + KIND[N1:N1 + t].count(kind), N1 + t)

            def layer2_products(n, s):
                pe.wait_ge(z1h_ready, n * SPB + (s + 2))
                for c in range(2):
                    last = nc.tensor.matmul(G[:, 0:QW], w2q[:, c, :], z1h[:, c * QW:(c + 1) * QW],
                                            start=(c == 0), stop=(c == 1))
                last.then_inc(g_done, 1)

            def tile_of(n, s, last, p):
                if p == 0:
                    pe.wait_ge(z1h_ready, n * SPB + (s + 1))
                if p == N1:
                    pe.wait_ge(d0_ready, n * SPB + (s + 2))
                tile(n * (SPB * KIND.count(KIND[p])), fixed(KIND[p], s, last, p), p)

            for p in range(PE_IN):
                tile_of(0, 0, False, p)

            def one_block(n, last):
                for s in range(SPB):
                    after = (s, N1 + 2) if more(s, last) else (s + 1, 1)
                    for here, p in window(s, last, PE_IN):
                        tile_of(n, here, last, p)
                        for q in AFTER.get(p, []) if here == s and more(s, last) else []:
                            if q == 0 and s + 2 == SPB:
                                pe.wait_ge(e_ready, n * READY + 2 * READY)
                            pe.wait_ge(t_evac, n * (SPB * GRP) + (s + 1) * GRP + (q + 1))
                            turn((s + 2) % SPB, q)
                        if (here, p) == after:
                            layer2_products(n, s)
                    if last and s == SPB - 1:
                        layer2_products(n, s)
                    pe.wait_ge(v_done, n * SPB + (s + 1))
                    nc.tensor.matmul(S[0:4, 0:QW], sel4[:, :], v2[:, :], start=True, stop=True)\
                        .then_inc(s_done, 1)

            with pe.Fori(0, NBLK - 1) as n:
                one_block(n, False)
            one_block(NBLK - 1, True)

            pe.wait_ge(z1h_ready, NSUP + 1)
            with pe.Fori(0, BATCH // HW) as c:
                per = HW // P
                pe.wait_ge(zs_ready, c * per + per)
                pe.wait_ge(zs_low, c * (per * SPB) + per * SPB)
                pe.wait_ge(zs_high, c * (per * SPB) + per * SPB)
                pe.wait_ge(dense_ready, c * per + per)
                for m in range(M1):
                    dst = (Z0, Z1)[m // 2][:, m % 2 * HW:(m % 2 + 1) * HW]
                    nc.tensor.matmul(dst, wt1a[:, m * P:(m + 1) * P], zs[:, bass.ds(c * HW, HW)],
                                     start=True, stop=False)
                    nc.tensor.matmul(dst, wt1b[:, m * P:(m + 1) * P], zsx[:, bass.ds(c * HW, HW)],
                                     start=False, stop=True).then_inc(top1_done, 1)
                for k in range(M1):
                    pe.wait_ge(h1_ready, c * M1 + (k + 1))
                    for m in range(M2):
                        last = nc.tensor.matmul(TP[:, m * HW:(m + 1) * HW], wt2[:, k, m * P:(m + 1) * P],
                                                h1[:, k, :], start=(k == 0), stop=(k == M1 - 1))
                        if k == M1 - 1:
                            last.then_inc(top2_done, 1)
                for k in range(M2):
                    pe.wait_ge(h2_ready, c * M2 + (k + 1))
                    last = nc.tensor.matmul(G[0:1, :], wt3[:, k:k + 1], h2[:, k, :],
                                            start=(k == 0), stop=(k == M2 - 1))
                last.then_inc(top3_done, 1)


_INS = (["dense_ctx", "ids"] + [f"tbl_{f}" for f in range(32)]
        + ["W_top1", "b_top1", "W_top2", "b_top2", "W_top3"]
        + [f"L0_rec_{w}" for w in ("W0", "b0", "W1", "b1", "W2", "b2")])


def kernel(**inputs):
    import numpy as _np
    import concourse.bacc as _bacc
    from concourse import mybir as _mybir
    from concourse.bass_utils import run_bass_kernel_spmd as _run

    nc = _bacc.Bacc("TRN2", target_bir_lowering=False, num_devices=1)
    arrays, aps = {}, {}
    for name in _INS:
        a = _np.ascontiguousarray(inputs[name])
        arrays[f"in_{name}"] = a
        aps[name] = nc.dram_tensor(f"in_{name}", a.shape, _mybir.dt.from_np(a.dtype), kind="ExternalInput").ap()
    batch = inputs["ids"].shape[0]
    out = nc.dram_tensor("out_y", (batch, 1), _mybir.dt.float32, kind="ExternalOutput").ap()
    build(nc, aps["dense_ctx"], aps["ids"], [aps[f"tbl_{f}"] for f in range(32)],
          *[aps[name] for name in _INS[34:]], out)
    r = _run(nc, [arrays], core_ids=[0])
    return r.results[0]["out_y"]
```
